# Optimizing a Trainium2 kernel written in Bass

```python
import numpy as np
import jax
import jax.numpy as jnp

def _softmax(x, axis=-1):
    return jax.nn.softmax(x, axis=axis)
def _gelu(x):
    return jax.nn.gelu(x, approximate=True)
def _silu(x):
    return jax.nn.silu(x)
def _sigmoid(x):
    return jax.nn.sigmoid(x)
def _layernorm(x, axis=-1, eps=1e-5):
    m = jnp.mean(x, axis=axis, keepdims=True)
    v = jnp.var(x, axis=axis, keepdims=True)
    return (x - m) / jnp.sqrt(v + eps)
def _scatter_add(tgt, idx, src, axis=0):
    return tgt.at[idx].add(src)
def _segment_sum(src, seg, n):
    return jax.ops.segment_sum(src, seg, n)

kernel_name = 'mk_conv_preact_d1_conv_nchw256_269d1e'

def setup_inputs(seed: int = 0):
    np.random.seed(seed)
    _w = jnp.asarray
    def _rec_inputs():
        import jax
        import jax.numpy as jnp
        _gk = jax.random.key(seed)
        x = -0.0003957 + 1 * jax.random.normal(jax.random.fold_in(_gk, 1), (16, 256, 56, 56), jnp.float32)
        return x
    x = _rec_inputs()
    def _L0_conv_setup():
        import jax, jax.numpy as jnp
        import numpy as np
        from jax import lax
        key = jax.random.key(seed)
        k1, k2, k3 = jax.random.split(key, 3)
        N, Cin, H, W = (16, 256, 56, 56)
        K, Cout, ks = (4, 256, 3)
        x = jax.random.normal(k1, (N, Cin, H, W), dtype=jnp.float32)
        weight = jax.random.normal(k2, (K, Cout, Cin, ks, ks), dtype=jnp.float32)
        att_w = jax.random.normal(k3, (K, Cin), dtype=jnp.float32) * 0.02
        att_b = jnp.zeros((K,), dtype=jnp.float32)
        return {'x': x, 'weight': weight, 'att_w': att_w, 'att_b': att_b}
    _L0_conv_all = _L0_conv_setup()
    _L0_conv_in = {k: v for k, v in _L0_conv_all.items() if k in ('weight', 'att_w', 'att_b', )}
    del _L0_conv_all

    return {
        "x": x,
        "L0_conv_weight": _L0_conv_in["weight"],
        "L0_conv_att_w": _L0_conv_in["att_w"],
        "L0_conv_att_b": _L0_conv_in["att_b"],
    }

def reference(x, L0_conv_weight, L0_conv_att_w, L0_conv_att_b):
    import jax
    import jax.numpy as jnp
    def _L0_conv_ref(x, weight, att_w, att_b):
        import jax, jax.numpy as jnp
        import numpy as np
        from jax import lax
        pooled = jnp.mean(x, axis=(2, 3))
        att = jax.nn.sigmoid(pooled @ att_w.T + att_b)
        agg_w = jnp.einsum('nk,kocij->nocij', att, weight)

        def conv_one(xi, wi):
            return lax.conv_general_dilated(xi[None], wi, window_strides=(1, 1), padding=[(1, 1), (1, 1)], dimension_numbers=('NCHW', 'OIHW', 'NCHW'))[0]
        out = jax.vmap(conv_one)(x, agg_w)
        return out

    def _gn(v, G=32, eps=1e-5):
        B_, C_, H_, W_ = v.shape
        g = v.reshape(B_, G, C_ // G, H_, W_)
        m = jnp.mean(g, axis=(2, 3, 4), keepdims=True)
        s = jnp.var(g, axis=(2, 3, 4), keepdims=True)
        return ((g - m) / jnp.sqrt(s + eps)).reshape(v.shape)

    def _ln_c(v, eps=1e-6):
        m = jnp.mean(v, axis=1, keepdims=True)
        s = jnp.var(v, axis=1, keepdims=True)
        return (v - m) / jnp.sqrt(s + eps)

    def _ln_t(v, eps=1e-5):
        m = jnp.mean(v, axis=-1, keepdims=True)
        s = jnp.var(v, axis=-1, keepdims=True)
        return (v - m) / jnp.sqrt(s + eps)

    def _to_tokens(v):
        B_, C_, H_, W_ = v.shape
        return v.reshape(B_, C_, H_ * W_).transpose(0, 2, 1)
    def _from_tokens(t, like):
        B_, C_, H_, W_ = like.shape
        return t.transpose(0, 2, 1).reshape(B_, C_, H_, W_)

    x = x + _L0_conv_ref(_gn(x), L0_conv_weight, L0_conv_att_w, L0_conv_att_b)
    return x


_drawn_inputs = setup_inputs


def setup_inputs(seed=0):
    import zlib

    import numpy as np

    out = dict(_drawn_inputs(seed))
    spreads = {'L0_conv_att_b': (0.0, 0.319)}
    factors = {'L0_conv_att_w': 21.764}
    for name, (base, spread) in spreads.items():
        noise = np.random.default_rng([zlib.crc32(name.encode()), seed]).standard_normal(out[name].shape)
        drawn = base * np.exp(spread * noise) if base else spread * noise
        out[name] = jnp.asarray(drawn.astype(out[name].dtype))
    for name, factor in factors.items():
        out[name] = (out[name] * factor).astype(out[name].dtype)
    return out
```

```python
from contextlib import ExitStack

import concourse.bass as bass
from concourse import mybir

P = 128
N, C, H, W = 16, 256, 56, 56
K, KS = 4, 3
CT = C // P
M = 4
NC = M + KS - 1
CH = 2
CR = H // CH
TR = CR // M
U = TR * W
HP = H + 2
VW = W + 1
VROW = TR * VW + 3
GS = 8
CI = 32
JT = P // CI
TAPS = KS * P
WG = CT * KS * TAPS
EPS = 1e-5

PA, PB = 0.75, 1.5
A2, B2 = PA * PA, PB * PB
F_0, F_A, F_B = A2 * B2, 2 * A2 * (A2 - B2), 2 * B2 * (B2 - A2)
POINT = [0.0, PA, -PA, PB, -PB, None]

V_SCALE = 64.0
ATT_SCALE = 2048.0
W_TOP = 2.0 ** 14
MIX_SCALE = 2.0 ** -14
F = [F_0, F_A, F_A, F_B, F_B, 1.0]
UNSCALE = 1.0 / (V_SCALE * ATT_SCALE * MIX_SCALE)

ALU = mybir.AluOpType
ACT = mybir.ActivationFunctionType
AX = mybir.AxisListType
F32 = mybir.dt.float32
F16 = mybir.dt.float16
I32 = mybir.dt.int32

SLOTS = CH * NC
GROUPS = SLOTS * CT
BANKS = 4
EB = 4

ITEMS = ([("V", 0, 0, 5)] + [("U", 0, c, 5) for c in range(CT)]
         + [("U", 0, c, j) for c in range(CT) for j in (3, 4)]
         + [("V", 0, 1, j) for j in range(NC)]
         + [("V", 1, 0, 0)] + [("U", 1, c, 0) for c in range(CT)]
         + [("V", 1, 0, 1), ("V", 1, 0, 2)]
         + [("U", 1, c, j) for c in range(CT) for j in (1, 2)]
         + [("V", 1, 0, 3), ("V", 1, 0, 4)])
NI = len(ITEMS)
INDEX = {it: n for n, it in enumerate(ITEMS)}


def buffered(it):
    return it[0] == "V" or it[3] in (1, 2, 3, 4)


E_ITEMS = [n for n, it in enumerate(ITEMS) if buffered(it)]
NE = len(E_ITEMS)
E_INDEX = {n: m for m, n in enumerate(E_ITEMS)}
FIRST_NEXT = INDEX[("V", 1, 0, 0)]
DVE_TAKES = [(k, o) for k in range(SLOTS) if k % NC in (0, 2, 4, 5) for o in range(CT)]
ACT_TAKES = [(k, o) for k in range(SLOTS) if k % NC in (1, 3) for o in range(CT)]
PAIRS = [(k, o) for k in range(SLOTS) if k % NC in (2, 4) for o in range(CT)]
MIX_UNITS = [(c, h) for c in range(CT) for h in range(CT)]
TAKES = KS * len(MIX_UNITS)


def conv_kernel(nc, x, w, att_w, att_b, out):
    x_dram = x.rearrange("n (c p) h w -> n p c (h w)", p=P)
    out_dram = out.rearrange("n (c p) h w -> n p c (h w)", p=P)

    with ExitStack() as ctx:
        def sb(name, shape, dt):
            return ctx.enter_context(nc.sbuf_tensor(name, shape, dt))

        def sem(name):
            return ctx.enter_context(nc.semaphore(name))

        X = [sb(f"X{b}", [P, CT, HP, W], F32) for b in range(2)]
        Vs = sb("Vs", [P, NC, 2, CT, VROW], F16)
        Us = sb("Us", [P, NC, 2, CT, CT, KS, P], F16)
        G = sb("G", [P, CT, CT, KS, TAPS], F32)
        W32 = sb("W32", [P, CT, JT, WG], F32)
        E = sb("E", [P, EB, CT * U], F32)
        T1 = sb("T1", [P, CT * U], F32)
        T2 = sb("T2", [P, CT * U], F32)
        SUM = sb("SUM", [P, CT, U], F32)
        DIF = sb("DIF", [P, CT, U], F32)
        avg = sb("avg", [P, P], F32)
        sel = sb("sel", [P, CI], F32)
        attw = sb("attw", [P, CT, P], F32)
        attb = sb("attb", [P, 1], F32)
        nattb = sb("nattb", [P, 1], F32)
        wmax = sb("wmax", [P, CT * JT], F32)
        wtop = sb("wtop", [P, 1], F32)
        wall = sb("wall", [P, 1], F32)
        ws = sb("ws", [P, 4], F32)
        us = sb("us", [P, NC + 2], F32)
        bn = sb("bn", [P, CT, 8, 6], F32)
        mv = sb("mv", [P, CT, 2], F32)
        mean = sb("mean", [P, 2, CT], F32)
        nmean = sb("nmean", [P, 2, CT], F32)
        rstd = sb("rstd", [P, CT], F32)
        stdm = sb("stdm", [P, 2, CT], F32)
        off = sb("off", [P, CT], F32)
        sq = sb("sq", [P, CT], F32)
        spread = sb("spread", [P, CT], F32)
        var = sb("var", [P, CT], F32)
        std0 = sb("std0", [P, CT], F32)
        rs0 = sb("rs0", [P, CT], F32)
        quo = sb("quo", [P, CT], F32)
        std = sb("std", [P, CT], F32)
        rs1 = sb("rs1", [P, CT], F32)
        pooled = sb("pooled", [P, CT], F32)
        ex = sb("ex", [P, 1], F32)
        ex1 = sb("ex1", [P, 1], F32)
        att = sb("att", [P, 1], F32)
        D32 = sb("D32", [P, CI], F32)
        D = sb("D", [P, 2, CI], F16)

        pM = ctx.enter_context(nc.psum_tensor("pM", [P, BANKS, 512], F32))
        pG = ctx.enter_context(nc.psum_tensor("pG", [P, KS, 512], F32))
        pS = ctx.enter_context(nc.psum_tensor("pS", [P, 512], F32))

        W16 = W32[:, :, :, :].bitcast(F16)
        stage = [X[1][:, i, 1:HP - 1, :].rearrange("p r w -> p (r w)")[:, 0:WG] for i in range(2)]

        w_in = [sem(f"w_in{c}") for c in range(CT * 2)]
        small_in = sem("small_in")
        x_in = [sem(f"x_in{c}") for c in range(CH)]
        stored = [sem(f"stored{c}") for c in range(CH)]
        pads_set = sem("pads_set")
        bias_set = sem("bias_set")
        avg_set = sem("avg_set")
        pool_step = sem("pool_step")
        w_top = sem("w_top")
        w_all = sem("w_all")
        w_scaled = sem("w_scaled")
        w_hi = sem("w_hi")
        w_lo_dve = sem("w_lo_dve")
        w_lo_pool = sem("w_lo_pool")
        pieces_ready = sem("pieces_ready")
        mean_ready = sem("mean_ready")
        spread_ready = sem("spread_ready")
        group_mean = sem("group_mean")
        group_var = sem("group_var")
        logits = sem("logits")
        shift_ready = sem("shift_ready")
        var_ready = sem("var_ready")
        std_ready = sem("std_ready")
        pooled_ready = sem("pooled_ready")
        exp_ready = sem("exp_ready")
        att_ready = sem("att_ready")
        centred = sem("centred")
        normed = sem("normed")
        mixed = sem("mixed")
        taps_taken = sem("taps_taken")
        comp_ready = sem("comp_ready")
        hi_done = sem("hi_done")
        lo_done = sem("lo_done")
        group_done = sem("group_done")
        restored = sem("restored")
        dve_took = sem("dve_took")
        act_took = sem("act_took")
        rows_added = sem("rows_added")
        row0_added = sem("row0_added")
        dve_step = sem("dve_step")

        def rows(b, chunk, i):
            r = CR * chunk + i
            return [X[b][:, c, r:r + M * (TR - 1) + 1:M, :] for c in range(CT)]

        def out_rows(b, chunk, o, r):
            q = CR * chunk + 1 + r
            return X[b][:, o, q:q + M * (TR - 1) + 1:M, :]

        def tiled(ap):
            return [ap[:, c * U:(c + 1) * U].rearrange("p (t w) -> p t w", w=W) for c in range(CT)]

        def tile_rows(ap):
            return ap.rearrange("p (t w) -> p t w", w=W)

        def comp_out(j, part, c):
            return Vs[:, j, part, c, 1:1 + TR * VW].rearrange("p (t w) -> p t w", w=VW)[:, :, 0:W]

        def comp_in(j, part, c, kx):
            return Vs[:, j, part, c, kx:kx + TR * VW].rearrange("p (t w) -> p t w", w=VW)[:, :, 0:W]

        def u_flat(j, part, c):
            return Us[:, j, part, c].rearrange("p o k n -> p o (k n)")

        def halves(ap):
            return ap[:, 0:CT * TAPS].rearrange("p (o n) -> p o n", o=CT)

        block = ctx.enter_context(nc.Block())

        @block.sync
        def _(sp):
            def load(n, b, chunk):
                src = x_dram[n] if isinstance(n, int) else x_dram[bass.ds(n, 1)].rearrange("n p c m -> (n p) c m")
                sp.dma_start(X[b][:, :, 1 + CR * chunk:1 + CR * (chunk + 1), :].rearrange("p c r w -> p c (r w)"),
                             src[:, :, CR * W * chunk:CR * W * (chunk + 1)]).then_inc(x_in[chunk], 16)

            def epoch(e, b, more):
                n = e - 1
                for chunk in range(CH):
                    sp.wait_ge(dve_took, e * len(DVE_TAKES) + len(DVE_TAKES) // 2 * (chunk + 1))
                    dst = out_dram[n] if isinstance(n, int) else out_dram[bass.ds(n, 1)].rearrange("n p c m -> (n p) c m")
                    sp.dma_start(dst[:, :, CR * W * chunk:CR * W * (chunk + 1)],
                                 X[b][:, :, 1 + CR * chunk:1 + CR * (chunk + 1), :].rearrange("p c r w -> p c (r w)")
                                 ).then_inc(stored[chunk], 16)
                    sp.wait_ge(stored[chunk], e * 16)
                    if more:
                        load(e + 1, b, chunk)

            for chunk in range(CH):
                load(0, 0, chunk)
            sp.dma_start(attw[:, :, :], att_w.rearrange("(c p) n -> p c n", p=P)).then_inc(small_in, 16)
            sp.dma_start(attb[:, :], att_b).then_inc(small_in, 16)
            for i in range(CT * 2):
                c, j = i // 2, JT // 2 * (i % 2)
                sp.dma_start(W32[:, c, j:j + JT // 2, :],
                             w[:, c * JT + j:c * JT + j + JT // 2, :]).then_inc(w_in[i], 16)
            sp.wait_ge(w_lo_dve, CT * JT // 2)
            sp.wait_ge(w_lo_pool, CT * JT // 2)
            for chunk in range(CH):
                load(1, 1, chunk)
            with sp.Fori(0, (N - 2) // 2) as i:
                epoch(i * 2 + 1, 0, True)
                epoch(i * 2 + 2, 1, True)
            epoch(N - 1, 0, False)
            epoch(N, 1, False)

        @block.tensor
        def _(pe):
            def group_mean_mm(e):
                pe.wait_ge(mean_ready, e + 1)
                pe.matmul(pS[:, 0:CT], avg[:, :], mv[:, :, 0], start=True, stop=True).then_inc(group_mean, 1)

            def group_var_mm(e):
                pe.wait_ge(spread_ready, e + 1)
                pe.matmul(pS[:, CT:2 * CT], avg[:, :], spread[:, :], start=True, stop=True).then_inc(group_var, 1)

            def logits_mm(e):
                pe.wait_ge(pooled_ready, e + 1)
                for c in range(CT):
                    mm = pe.matmul(pS[:, 2 * CT:2 * CT + 1], attw[:, c, :], pooled[:, c:c + 1],
                                   start=(c == 0), stop=(c == CT - 1))
                mm.then_inc(logits, 1)

            def mix(e, u):
                c, h = MIX_UNITS[u]
                if u == 0:
                    pe.wait_ge(att_ready, e + 1)
                for ky in range(KS):
                    pe.wait_ge(taps_taken, e * TAKES + TAKES + KS * (u - 1) + ky + 1)
                    for a, b in ((0, 0), (0, 1), (1, 0)):
                        for j in range(JT):
                            at = b * WG + (h * KS + ky) * TAPS
                            mm = pe.matmul(pG[CI * j:CI * (j + 1), ky, 0:TAPS], D[:, a, :],
                                           W16[:, c, j, at:at + TAPS], start=(a == 0 and b == 0), stop=(a == 1),
                                           tile_position=(0, CI * j))
                    mm.then_inc(mixed, 1)

            def group(e, k, o):
                chunk, j = k // NC, k % NC
                g = CT * k + o
                if o == 0:
                    v, u = ("V", 0, chunk, j), ("U", 0, CT - 1, j)
                    need = [INDEX[i] + 1 if i in INDEX else INDEX[(i[0], 1) + i[2:]] + 1 - NI
                            for i in ((v, u) if chunk == 0 else (v,))]
                    pe.wait_ge(lo_done, e * NI + max(need))
                before = ((k - 2) % SLOTS, o)
                past = len(ACT_TAKES if before in ACT_TAKES else DVE_TAKES) if k < 2 else 0
                if before in ACT_TAKES:
                    pe.wait_ge(act_took, e * len(ACT_TAKES) - past + ACT_TAKES.index(before) + 1)
                else:
                    pe.wait_ge(dve_took, e * len(DVE_TAKES) - past + DVE_TAKES.index(before) + 1)
                n = 0
                for c in range(CT):
                    for kx in range(KS):
                        for a, b in ((0, 0), (0, 1), (1, 0)):
                            mm = pe.matmul(pM[:, g % BANKS, 0:U].rearrange("p (t w) -> p t w", w=W),
                                           Us[:, j, a, c, o, kx, :], comp_in(j, b, c, kx),
                                           start=(n == 0), stop=(n == 3 * KS * CT - 1))
                            n += 1
                mm.then_inc(group_done, 1)

            def epoch(e, more):
                for k in range(SLOTS):
                    for o in range(CT):
                        group(e, k, o)
                        if more:
                            if (k, o) == (3, 1):
                                group_mean_mm(e)
                            if (k, o) == (4, 0):
                                group_var_mm(e)
                            if (k, o) == (5, 0):
                                logits_mm(e)
                            if (5, 1) <= (k, o) <= (7, 0):
                                mix(e, CT * k + o - 11)

            pe.sem_inc(group_done, GROUPS)
            pe.wait_ge(avg_set, 1)
            group_mean_mm(0)
            group_var_mm(0)
            pe.wait_ge(small_in, 32)
            logits_mm(0)
            pe.wait_ge(w_lo_dve, CT * JT // 2)
            pe.wait_ge(w_lo_pool, CT * JT // 2)
            for u in range(len(MIX_UNITS)):
                mix(0, u)
            pe.wait_ge(pads_set, 1)
            with pe.Fori(0, (N - 2) // 2) as i:
                epoch(i * 2 + 1, True)
                epoch(i * 2 + 2, True)
            epoch(N - 1, True)
            epoch(N, False)

        @block.vector
        def _(dve):
            steps, first = [0], [0]

            def step(e, ins):
                steps[0] += 1
                ins.then_inc(dve_step, 1)
                dve.wait_ge(dve_step, (e - 1) * STEPS + first[0] + steps[0])

            def buffer_free(e, n):
                m = E_INDEX[n] - EB
                last = E_ITEMS[m] if m >= 0 else E_ITEMS[m + NE] - NI
                dve.wait_ge(lo_done, e * NI + last + 1)
                return E[:, E_INDEX[n] % EB, :]

            def temps_free(e, n):
                dve.wait_ge(comp_ready, e * NE + E_INDEX[n])

            def combine(dst, a, scale, d):
                for c in range(CT):
                    ins = dve.scalar_tensor_tensor(out=dst[c], in0=a[c], scalar=scale, in1=d[c],
                                                   op0=ALU.mult, op1=ALU.add)
                return ins

            def v_single(e, b, n):
                _, _, chunk, j = ITEMS[n]
                i = 0 if j == 0 else 1
                t1 = tiled(T1)
                temps_free(e, n)
                step(e, combine(t1, rows(b, chunk, i + 2), -(A2 + B2), rows(b, chunk, i + 4)))
                dst = tiled(buffer_free(e, n))
                combine(dst, rows(b, chunk, i), A2 * B2, t1).then_inc(comp_ready, 1)

            def v_pair(e, b, n):
                _, _, chunk, j = ITEMS[n]
                q2 = B2 if j == 1 else A2
                temps_free(e, n)
                combine(tiled(T1), rows(b, chunk, 2), -q2, rows(b, chunk, 4))
                step(e, combine(tiled(T2), rows(b, chunk, 1), -q2, rows(b, chunk, 3)))
                for m in range(2):
                    dst = buffer_free(e, n + m)
                    dve.scalar_tensor_tensor(out=dst, in0=T2[:, :], scalar=POINT[j + m], in1=T1[:, :],
                                             op0=ALU.mult, op1=ALU.add).then_inc(comp_ready, 1)

            def u_pair(e, n):
                j = ITEMS[n][3]
                p = POINT[j]
                temps_free(e, n)
                for c, t in enumerate((T1, T2)):
                    ins = dve.scalar_tensor_tensor(out=halves(t), in0=G[:, c, :, 2, :], scalar=p * p,
                                                   in1=G[:, c, :, 0, :], op0=ALU.mult, op1=ALU.add)
                step(e, ins)
                for c, t in enumerate((T1, T2)):
                    for m in range(2):
                        dst = buffer_free(e, n + 2 * c + m)
                        dve.scalar_tensor_tensor(out=halves(dst), in0=G[:, c, :, 1, :], scalar=POINT[j + m],
                                                 in1=halves(t), op0=ALU.mult, op1=ALU.add).then_inc(comp_ready, 1)

            def stats(e, b, chunk):
                if not (isinstance(e, int) and e == 0):
                    dve.wait_ge(mean_ready, e)
                dve.wait_ge(x_in[chunk], e * 16 + 16)
                for c in range(CT):
                    for q in range(4):
                        r = 1 + CR * chunk + TR * q
                        ins = dve.bn_stats(bn[:, c, 4 * chunk + q, :],
                                           X[b][:, c, r:r + TR, :].rearrange("p r w -> p (r w)"))
                return ins

            def channel_stats(e):
                for c in range(CT):
                    ins = dve.bn_aggr(mv[:, c, :], bn[:, c].rearrange("p q s -> p (q s)"))
                ins.then_inc(mean_ready, 1)

            def group_shift(e, b):
                dve.wait_ge(group_mean, e + 1)
                dve.tensor_scalar(mean[:, b, :], pS[:, 0:CT], 1.0, None, ALU.mult)
                ins = dve.tensor_scalar(nmean[:, b, :], pS[:, 0:CT], -1.0, None, ALU.mult)
                ins.then_inc(shift_ready, 1)
                dve.wait_ge(shift_ready, e + 1)
                step(e, dve.tensor_tensor(off[:, :], mv[:, :, 0], nmean[:, b, :], ALU.add))
                step(e, dve.tensor_tensor(sq[:, :], off[:, :], off[:, :], ALU.mult))
                dve.tensor_tensor(spread[:, :], sq[:, :], mv[:, :, 1], ALU.add).then_inc(spread_ready, 1)

            def group_variance(e):
                dve.wait_ge(group_var, e + 1)
                dve.tensor_scalar(var[:, :], pS[:, CT:2 * CT], EPS, None, ALU.add).then_inc(var_ready, 1)

            def norm_scale(e, b):
                dve.wait_ge(std_ready, e + 1)
                step(e, dve.reciprocal(rs0[:, :], std0[:, :]))
                step(e, dve.tensor_tensor(quo[:, :], var[:, :], rs0[:, :], ALU.mult))
                step(e, dve.tensor_tensor(std[:, :], quo[:, :], std0[:, :], ALU.add))
                step(e, dve.reciprocal(rs1[:, :], std[:, :]))
                dve.tensor_scalar(stdm[:, b, :], std[:, :], 0.5 / V_SCALE, None, ALU.mult)
                dve.tensor_scalar(rstd[:, :], rs1[:, :], 2.0 * V_SCALE, None, ALU.mult)
                dve.scalar_tensor_tensor(out=pooled[:, :], in0=off[:, :], scalar=2.0, in1=rs1[:, :],
                                         op0=ALU.mult, op1=ALU.mult).then_inc(pooled_ready, 1)

            def attention(e):
                dve.wait_ge(exp_ready, e + 1)
                step(e, dve.tensor_scalar(ex1[:, :], ex[:, :], 1.0, None, ALU.add))
                step(e, dve.reciprocal(att[:, :], ex1[:, :]))
                step(e, dve.tensor_scalar(D32[:, :], sel[:, :], att[:, 0:1], ATT_SCALE, ALU.mult, ALU.mult))
                dve.wait_ge(mixed, e * TAKES)
                step(e, dve.tensor_copy(D[:, 0, :], D32[:, :]))
                dve.tensor_tensor(D[:, 1, :], D32[:, :], D[:, 0, :], ALU.subtract).then_inc(att_ready, 1)

            def take(e, b, k, o):
                chunk, j = k // NC, k % NC
                g = CT * k + o
                res = pM[:, g % BANKS, 0:U]
                dve.wait_ge(group_done, e * GROUPS + g + 1)
                if j in (0, 5):
                    r = 0 if j == 0 else M - 1
                    if j == 0:
                        dve.wait_ge(restored, e * 6 + (2 if chunk == 0 else 6))
                    else:
                        dve.wait_ge(rows_added, e * len(PAIRS) + PAIRS.index((k - 1, o)) + 1)
                        if o == CT - 1:
                            dve.wait_ge(row0_added, e * len(PAIRS) + PAIRS.index((k - 1, o)) + 1)
                    y = out_rows(b, chunk, o, r)
                    dve.scalar_tensor_tensor(out=y, in0=tile_rows(res), scalar=us[:, j:j + 1], in1=y,
                                             op0=ALU.mult, op1=ALU.add).then_inc(dve_took, 1)
                    return
                dve.wait_ge(act_took, e * len(ACT_TAKES) + ACT_TAKES.index((k - 1, o)) + 1)
                dve.wait_ge(row0_added, e * len(PAIRS) + PAIRS.index((k, o)) + 1 - CT)
                step(e, dve.scalar_tensor_tensor(out=SUM[:, o, :], in0=res, scalar=us[:, j:j + 1],
                                                 in1=DIF[:, o, :], op0=ALU.mult, op1=ALU.add))
                dve.scalar_tensor_tensor(out=DIF[:, o, :], in0=res, scalar=us[:, NC + j // 2 - 1:NC + j // 2],
                                         in1=DIF[:, o, :], op0=ALU.mult, op1=ALU.add).then_inc(dve_took, 1)
                if j == 2:
                    dve.wait_ge(restored, e * 6 + (4 if chunk == 0 else 6))
                dve.wait_ge(dve_took, e * len(DVE_TAKES) + DVE_TAKES.index((k, o)) + 1)
                for r in (2, 1, 3):
                    y = out_rows(b, chunk, o, r)
                    src = (DIF if r % 2 else SUM)[:, o, :]
                    ins = dve.scalar_tensor_tensor(out=y, in0=tile_rows(src), scalar=POINT[j - 1] ** r, in1=y,
                                                   op0=ALU.mult, op1=ALU.add)
                ins.then_inc(rows_added, 1)

            def epoch(e, b, more):
                steps[0] = 0
                for k in range(SLOTS):
                    if k == 0:
                        v_single(e, b, INDEX[("V", 0, 0, 5)])
                        u_pair(e, INDEX[("U", 0, 0, 3)])
                    if k == 1:
                        v_single(e, b, INDEX[("V", 0, 1, 0)])
                        if more:
                            stats(e, 1 - b, 0)
                    if k == 3:
                        if more:
                            stats(e, 1 - b, 1).then_inc(pieces_ready, 1)
                            dve.wait_ge(pieces_ready, e + 1)
                        v_pair(e, b, INDEX[("V", 0, 1, 1)])
                        if more:
                            channel_stats(e)
                    if k == 5:
                        v_pair(e, b, INDEX[("V", 0, 1, 3)])
                    if k == 6:
                        v_single(e, b, INDEX[("V", 0, 1, 5)])
                    if more:
                        if k == 4:
                            group_shift(e, 1 - b)
                        if k == 7:
                            dve.wait_ge(normed, e * 4 + 4)
                            v_single(e, 1 - b, INDEX[("V", 1, 0, 0)])
                        if k == 9:
                            v_pair(e, 1 - b, INDEX[("V", 1, 0, 1)])
                        if k == 10:
                            dve.wait_ge(taps_taken, e * TAKES + 2 * TAKES)
                            u_pair(e, INDEX[("U", 1, 0, 1)])
                        if k == 11:
                            v_pair(e, 1 - b, INDEX[("V", 1, 0, 3)])
                    for o in range(CT):
                        if (k, o) in DVE_TAKES:
                            take(e, b, k, o)
                        if more and (k, o) == (4, 0):
                            group_variance(e)
                        if more and (k, o) == (4, 1):
                            norm_scale(e, 1 - b)
                        if more and (k, o) == (5, 0):
                            attention(e)
                assert steps[0] == STEPS or not more, steps

            def prepare_first():
                stats(0, 0, 1).then_inc(pieces_ready, 1)
                dve.wait_ge(pieces_ready, 1)
                channel_stats(0)
                group_shift(0, 0)
                group_variance(0)
                norm_scale(0, 0)

            def prepare_first_components():
                dve.wait_ge(avg_set, 1)
                attention(0)
                dve.wait_ge(normed, 4)
                v_single(0, 0, INDEX[("V", 1, 0, 0)])
                v_pair(0, 0, INDEX[("V", 1, 0, 1)])
                dve.wait_ge(taps_taken, 2 * TAKES)
                u_pair(0, INDEX[("U", 1, 0, 1)])
                v_pair(0, 0, INDEX[("V", 1, 0, 3)])

            STEPS = 28
            first[0] = STEPS
            dve.sem_inc(dve_took, len(DVE_TAKES))
            dve.sem_inc(comp_ready, E_INDEX[FIRST_NEXT])
            dve.sem_inc(rows_added, len(PAIRS))
            for b in range(2):
                dve.memset(X[b][:, :, 0:1, :], 0.0)
                dve.memset(X[b][:, :, HP - 1:HP, :], 0.0)
            dve.memset(Vs[:, :, :, :, 0:VW * TR + 1:VW].rearrange("p j s c m -> p (j s c) m"), 0.0).then_inc(pads_set, 1)
            dve.wait_ge(pads_set, 1)
            stats(0, 0, 0)
            prepare_first()
            for i in range(CT * JT):
                if i % 2 == 0:
                    dve.wait_ge(w_in[i // 2], 16)
                ins = dve.tensor_reduce(wmax[:, i:i + 1], W32[:, i // JT, i % JT, :], AX.X, ALU.max,
                                        apply_absolute_value=True)
            step(0, ins)
            dve.tensor_reduce(wtop[:, :], wmax[:, :], AX.X, ALU.max).then_inc(w_top, 1)
            dve.wait_ge(w_all, 1)
            step(0, dve.tensor_scalar(ws[:, 0:1], wall[:, :], 2.0 ** -100, None, ALU.max))
            step(0, dve.reciprocal(ws[:, 1:2], ws[:, 0:1]))
            step(0, dve.tensor_scalar(ws[:, 2:3], ws[:, 1:2], W_TOP, None, ALU.mult))
            step(0, dve.tensor_scalar(ws[:, 2:3].bitcast(I32), ws[:, 2:3].bitcast(I32), 0x7F800000, None,
                                      ALU.bitwise_and))
            step(0, dve.reciprocal(ws[:, 3:4], ws[:, 2:3]))
            for j in range(NC):
                dve.tensor_scalar(us[:, j:j + 1], ws[:, 3:4], UNSCALE / F[j], None, ALU.mult)
            for j in (2, 4):
                dve.tensor_scalar(us[:, NC + j // 2 - 1:NC + j // 2], ws[:, 3:4], -UNSCALE / F[j], None, ALU.mult)

            def w_lo(i):
                dve.wait_ge(w_hi, i + 1)
                dve.tensor_tensor(W16[:, i // JT, i % JT, WG:2 * WG], stage[i % 2],
                                  W16[:, i // JT, i % JT, 0:WG], ALU.subtract).then_inc(w_lo_dve, 1)

            for i in range(CT * JT):
                if i >= 2 and i % 2 == 1:
                    dve.wait_ge(w_lo_pool, i // 2)
                if i >= 2 and i % 2 == 0:
                    dve.wait_ge(w_lo_dve, i // 2)
                dve.tensor_scalar(stage[i % 2], W32[:, i // JT, i % JT, :], ws[:, 2:3], None,
                                  ALU.mult).then_inc(w_scaled, 1)
                if i % 2 == 1:
                    w_lo(i - 1)
            prepare_first_components()
            first[0] = steps[0]
            with dve.Fori(0, (N - 2) // 2) as i:
                epoch(i * 2 + 1, 0, True)
                epoch(i * 2 + 2, 1, True)
            epoch(N - 1, 0, True)
            epoch(N, 1, False)

        @block.scalar
        def _(act):
            def hi(e, n):
                kind, nxt, c, j = ITEMS[n]
                if n == 0:
                    act.wait_ge(group_done, e * GROUPS)
                elif kind == "V" and nxt == 0:
                    act.wait_ge(group_done, e * GROUPS + CT * (j + 1))
                elif nxt == 1:
                    act.wait_ge(group_done, e * GROUPS + CT * (NC + j + 1))
                if kind == "U" and j == 0:
                    act.wait_ge(taps_taken, e * TAKES + TAKES + KS * CT * (c + 1))
                if buffered(ITEMS[n]):
                    act.wait_ge(comp_ready, e * NE + E_INDEX[n] + 1)
                if kind == "V":
                    for t in range(CT):
                        ins = act.copy(comp_out(j, 0, t), tile_rows(E[:, E_INDEX[n] % EB, t * U:(t + 1) * U]))
                else:
                    src = halves(E[:, E_INDEX[n] % EB, :]) if buffered(ITEMS[n]) else G[:, c, :, 0 if j == 0 else 2, :]
                    ins = act.copy(u_flat(j, 0, c), src)
                ins.then_inc(hi_done, 1)

            def take(e, k, o):
                g = CT * k + o
                act.wait_ge(group_done, e * GROUPS + g + 1)
                act.wait_ge(rows_added, e * len(PAIRS) + PAIRS.index((k + 1, o)) + 1 - CT)
                act.activation(DIF[:, o, :], pM[:, g % BANKS, 0:U], ACT.Identity,
                               scale=us[:, k % NC:k % NC + 1]).then_inc(act_took, 1)

            def take_taps(e, u):
                c, h = MIX_UNITS[u]
                if u == 0:
                    act.wait_ge(lo_done, e * NI + INDEX[("U", 0, 1, 4)] + 1)
                for ky in range(KS):
                    act.wait_ge(mixed, e * TAKES + KS * u + ky + 1)
                    act.mul(G[:, c, h, ky, :], pG[:, ky, 0:TAPS], MIX_SCALE).then_inc(taps_taken, 1)

            def restore(e, b, first, last):
                for c in range(CT):
                    y = X[b][:, c, first:last, :]
                    act.activation(y, y, ACT.Identity, bias=mean[:, b, c:c + 1],
                                   scale=stdm[:, b, c:c + 1]).then_inc(restored, 1)

            def centre(e, b):
                act.wait_ge(shift_ready, e + 1)
                for chunk in range(CH):
                    for c in range(CT):
                        y = X[b][:, c, 1 + CR * chunk:1 + CR * (chunk + 1), :]
                        act.activation(y, y, ACT.Identity, bias=nmean[:, b, c:c + 1]).then_inc(centred, 1)

            def norm(e, b):
                act.wait_ge(pooled_ready, e + 1)
                for chunk in range(CH):
                    for c in range(CT):
                        act.wait_ge(centred, e * 4 + CT * chunk + c + 1)
                        y = X[b][:, c, 1 + CR * chunk:1 + CR * (chunk + 1), :]
                        act.activation(y, y, ACT.Copy, scale=rstd[:, c:c + 1]).then_inc(normed, 1)

            def root(e):
                act.wait_ge(var_ready, e + 1)
                act.activation(std0[:, :], var[:, :], ACT.Sqrt).then_inc(std_ready, 1)

            def exponential(e):
                act.wait_ge(logits, e + 1)
                act.activation(ex[:, :], pS[:, 2 * CT:2 * CT + 1], ACT.Exp, bias=nattb[:, 0:1],
                               scale=-1.0).then_inc(exp_ready, 1)

            def epoch(e, b, more):
                for k in range(SLOTS):
                    if k == 0:
                        hi(e, INDEX[("V", 0, 0, 5)])
                        restore(e, b, 1, CR)
                        for n in range(INDEX[("U", 0, 0, 5)], INDEX[("U", 0, 1, 4)] + 1):
                            hi(e, n)
                    if k == 1:
                        hi(e, INDEX[("V", 0, 1, 0)])
                        restore(e, b, CR, CR + 1)
                    if k == 3:
                        for j in (1, 2):
                            hi(e, INDEX[("V", 0, 1, j)])
                    if k == 4 and more:
                        centre(e, 1 - b)
                        root(e)
                    if k == 5:
                        for j in (3, 4):
                            hi(e, INDEX[("V", 0, 1, j)])
                    if k == 6:
                        hi(e, INDEX[("V", 0, 1, 5)])
                        if more:
                            take_taps(e, 0)
                        restore(e, b, CR + 1, H + 1)
                    if more:
                        if k == 5:
                            exponential(e)
                            norm(e, 1 - b)
                        if k == 6:
                            take_taps(e, 1)
                        if k == 7:
                            take_taps(e, 2)
                            hi(e, INDEX[("V", 1, 0, 0)])
                            hi(e, INDEX[("U", 1, 0, 0)])
                        if k == 9:
                            for j in (1, 2):
                                hi(e, INDEX[("V", 1, 0, j)])
                        if k == 10:
                            for c in range(CT):
                                for j in (1, 2):
                                    hi(e, INDEX[("U", 1, c, j)])
                        if k == 11:
                            for j in (3, 4):
                                hi(e, INDEX[("V", 1, 0, j)])
                    for o in range(CT):
                        if (k, o) in ACT_TAKES:
                            take(e, k, o)
                        if more and (k, o) == (7, 0):
                            take_taps(e, 3)
                            hi(e, INDEX[("U", 1, 1, 0)])

            act.sem_inc(act_took, len(ACT_TAKES))
            act.sem_inc(hi_done, FIRST_NEXT)
            act.sem_inc(restored, 6)
            act.sem_inc(taps_taken, TAKES)
            act.wait_ge(small_in, 32)
            act.mul(nattb[:, :], attb[:, :], -1.0).then_inc(bias_set, 1)
            centre(0, 0)
            root(0)
            act.wait_ge(bias_set, 1)
            exponential(0)
            norm(0, 0)
            for i in range(CT * JT):
                act.wait_ge(w_scaled, i + 1)
                act.copy(W16[:, i // JT, i % JT, 0:WG], stage[i % 2]).then_inc(w_hi, 1)
            for u in range(len(MIX_UNITS)):
                take_taps(0, u)
            for n in range(FIRST_NEXT, NI):
                hi(0, n)
            with act.Fori(0, (N - 2) // 2) as i:
                epoch(i * 2 + 1, 0, True)
                epoch(i * 2 + 2, 1, True)
            epoch(N - 1, 0, True)
            epoch(N, 1, False)

        @block.gpsimd
        def _(pool):
            def lo(e, n):
                kind, nxt, c, j = ITEMS[n]
                pool.wait_ge(hi_done, e * NI + n + 1)
                if kind == "V":
                    for t in range(CT):
                        ins = pool.tensor_tensor(comp_out(j, 1, t), tile_rows(E[:, E_INDEX[n] % EB, t * U:(t + 1) * U]),
                                                 comp_out(j, 0, t), ALU.subtract)
                else:
                    src = halves(E[:, E_INDEX[n] % EB, :]) if buffered(ITEMS[n]) else G[:, c, :, 0 if j == 0 else 2, :]
                    ins = pool.tensor_tensor(u_flat(j, 1, c), src, u_flat(j, 0, c), ALU.subtract)
                ins.then_inc(lo_done, 1)

            def add(e, b, k, o):
                pool.wait_ge(dve_took, e * len(DVE_TAKES) + DVE_TAKES.index((k, o)) + 1)
                if k % NC == 4:
                    pool.wait_ge(row0_added, e * len(PAIRS) + PAIRS.index((k, o)) + 1 - CT)
                y = out_rows(b, k // NC, o, 0)
                pool.tensor_tensor(y, y, tile_rows(SUM[:, o, :]), ALU.add).then_inc(row0_added, 1)

            def epoch(e, b, more):
                for k in range(SLOTS):
                    if k == 0:
                        for n in range(0, INDEX[("U", 0, 1, 4)] + 1):
                            lo(e, n)
                    if k == 1:
                        lo(e, INDEX[("V", 0, 1, 0)])
                    if k == 3:
                        for j in (1, 2):
                            lo(e, INDEX[("V", 0, 1, j)])
                    if k == 5:
                        for j in (3, 4):
                            lo(e, INDEX[("V", 0, 1, j)])
                    if k == 6:
                        lo(e, INDEX[("V", 0, 1, 5)])
                    if more:
                        if k == 7:
                            for n in range(FIRST_NEXT, INDEX[("U", 1, 1, 0)] + 1):
                                lo(e, n)
                        if k == 9:
                            for j in (1, 2):
                                lo(e, INDEX[("V", 1, 0, j)])
                        if k == 10:
                            for c in range(CT):
                                for j in (1, 2):
                                    lo(e, INDEX[("U", 1, c, j)])
                        if k == 11:
                            for j in (3, 4):
                                lo(e, INDEX[("V", 1, 0, j)])
                    for o in range(CT):
                        if k % NC in (2, 4):
                            add(e, b, k, o)

            pool.sem_inc(lo_done, FIRST_NEXT)
            pool.sem_inc(row0_added, len(PAIRS))
            pool.memset(sel[:, :], 0.0).then_inc(pool_step, 1)
            pool.wait_ge(pool_step, 1)
            for k in range(K):
                pool.affine_select(out=sel[:, :], in_=sel[:, :], compare_op=ALU.not_equal, fill=1.0, base=-CI * k,
                                   pattern=[[-1, CI]], channel_multiplier=1).then_inc(pool_step, 1)
                pool.wait_ge(pool_step, k + 2)
            blocks = avg[:, :].rearrange("p (g j) -> p g j", j=GS)
            pool.memset(avg[:, :], 1.0 / GS).then_inc(pool_step, 1)
            pool.wait_ge(pool_step, K + 2)
            pool.affine_select(out=blocks, in_=blocks, compare_op=ALU.is_ge, fill=0.0, base=0,
                               pattern=[[-GS, P // GS], [0, GS]], channel_multiplier=1).then_inc(pool_step, 1)
            pool.wait_ge(pool_step, K + 3)
            pool.affine_select(out=blocks, in_=blocks, compare_op=ALU.is_ge, fill=0.0, base=GS - 1,
                               pattern=[[GS, P // GS], [0, GS]], channel_multiplier=-1).then_inc(avg_set, 1)
            pool.wait_ge(w_top, 1)
            pool.partition_all_reduce(wall[:, :], wtop[:, :], P, bass.bass_isa.ReduceOp.max).then_inc(w_all, 1)
            for i in range(1, CT * JT, 2):
                pool.wait_ge(w_hi, i + 1)
                pool.tensor_tensor(W16[:, i // JT, i % JT, WG:2 * WG], stage[1],
                                   W16[:, i // JT, i % JT, 0:WG], ALU.subtract).then_inc(w_lo_pool, 1)
            for n in range(FIRST_NEXT, NI):
                lo(0, n)
            with pool.Fori(0, (N - 2) // 2) as i:
                epoch(i * 2 + 1, 0, True)
                epoch(i * 2 + 2, 1, True)
            epoch(N - 1, 0, True)
            epoch(N, 1, False)


def kernel(x, L0_conv_weight, L0_conv_att_w, L0_conv_att_b):
    import numpy as np
    import concourse.bacc as bacc
    from concourse.bass_utils import run_bass_kernel_spmd

    nc = bacc.Bacc("TRN2", target_bir_lowering=False, num_devices=1, dynamic_dma_scratch_size=16)
    w = np.ascontiguousarray(L0_conv_weight).reshape(K, CT, P, CT, JT, CI, KS, KS)
    w = np.ascontiguousarray(w.transpose(0, 5, 3, 4, 1, 6, 7, 2)).reshape(P, CT * JT, WG)
    arrays = {
        "x_dram": np.ascontiguousarray(x),
        "w_dram": w,
        "attw_dram": np.repeat(np.ascontiguousarray(L0_conv_att_w).T, CI, axis=1),
        "attb_dram": np.repeat(np.ascontiguousarray(L0_conv_att_b), CI).reshape(P, 1),
    }
    args = [nc.dram_tensor(n, a.shape, F32, kind="ExternalInput").ap() for n, a in arrays.items()]
    args.append(nc.dram_tensor("out_dram", (N, C, H, W), F32, kind="ExternalOutput").ap())
    conv_kernel(nc, *args)
    return run_bass_kernel_spmd(nc, [arrays], core_ids=[0]).results[0]["out_dram"]
```

```python
from contextlib import ExitStack

import concourse.bass as bass
from concourse import mybir

P = 128
N, C, H, W = 16, 256, 56, 56
K, KS = 4, 3
CT = C // P
M = 4
NC = M + KS - 1
CH = 2
CR = H // CH
TR = CR // M
U = TR * W
HP = H + 2
VW = W + 1
VROW = TR * VW + 3
GS = 8
CI = 32
JT = P // CI
TAPS = KS * P
WG = CT * KS * TAPS
EPS = 1e-5

PA, PB = 0.75, 1.5
A2, B2 = PA * PA, PB * PB
F_0, F_A, F_B = A2 * B2, 2 * A2 * (A2 - B2), 2 * B2 * (B2 - A2)
POINT = [0.0, PA, -PA, PB, -PB, None]

V_SCALE = 64.0
ATT_SCALE = 2048.0
W_TOP = 2.0 ** 14
MIX_SCALE = 2.0 ** -14
F = [F_0, F_A, F_A, F_B, F_B, 1.0]
UNSCALE = 1.0 / (V_SCALE * ATT_SCALE * MIX_SCALE)

ALU = mybir.AluOpType
ACT = mybir.ActivationFunctionType
AX = mybir.AxisListType
F32 = mybir.dt.float32
F16 = mybir.dt.float16
I32 = mybir.dt.int32

SLOTS = CH * NC
GROUPS = SLOTS * CT
BANKS = 4
EB = 4

ITEMS = ([("V", 0, 0, 5)] + [("U", 0, c, j) for c in range(CT) for j in (3, 4)]
         + [("U", 0, c, 5) for c in range(CT)]
         + [("V", 0, 1, j) for j in range(NC)]
         + [("V", 1, 0, 0)] + [("U", 1, c, 0) for c in range(CT)]
         + [("V", 1, 0, 1), ("V", 1, 0, 2)]
         + [("U", 1, c, j) for c in range(CT) for j in (1, 2)]
         + [("V", 1, 0, 3), ("V", 1, 0, 4)])
NI = len(ITEMS)
INDEX = {it: n for n, it in enumerate(ITEMS)}


def buffered(it):
    return it[0] == "V" or it[3] in (1, 2, 3, 4)


E_ITEMS = [n for n, it in enumerate(ITEMS) if buffered(it)]
NE = len(E_ITEMS)
E_INDEX = {n: m for m, n in enumerate(E_ITEMS)}
FIRST_NEXT = INDEX[("V", 1, 0, 0)]
DVE_TAKES = [(k, o) for k in range(SLOTS) if k % NC in (0, 2, 4, 5) for o in range(CT)]
ACT_TAKES = [(k, o) for k in range(SLOTS) if k % NC in (1, 3) for o in range(CT)]
PAIRS = [(k, o) for k in range(SLOTS) if k % NC in (2, 4) for o in range(CT)]
MIX_UNITS = [(c, h) for c in range(CT) for h in range(CT)]
TAKES = KS * len(MIX_UNITS)


def conv_kernel(nc, x, w, att_w, att_b, out):
    x_dram = x.rearrange("n (c p) h w -> n p c (h w)", p=P)
    out_dram = out.rearrange("n (c p) h w -> n p c (h w)", p=P)

    with ExitStack() as ctx:
        def sb(name, shape, dt):
            return ctx.enter_context(nc.sbuf_tensor(name, shape, dt))

        def sem(name):
            return ctx.enter_context(nc.semaphore(name))

        X = [sb(f"X{b}", [P, CT, HP, W], F32) for b in range(2)]
        Vs = sb("Vs", [P, NC, 2, CT, VROW], F16)
        Us = sb("Us", [P, NC, 2, CT, CT, KS, P], F16)
        G = sb("G", [P, CT, CT, KS, TAPS], F32)
        W32 = sb("W32", [P, CT, JT, WG], F32)
        E = sb("E", [P, EB, CT * U], F32)
        T1 = sb("T1", [P, CT * U], F32)
        T2 = sb("T2", [P, CT * U], F32)
        SUM = sb("SUM", [P, CT, U], F32)
        DIF = sb("DIF", [P, CT, U], F32)
        avg = sb("avg", [P, P], F32)
        sel = sb("sel", [P, CI], F32)
        attw = sb("attw", [P, CT, P], F32)
        attb = sb("attb", [P, 1], F32)
        nattb = sb("nattb", [P, 1], F32)
        wmax = sb("wmax", [P, CT * JT], F32)
        wtop = sb("wtop", [P, 1], F32)
        wall = sb("wall", [P, 1], F32)
        ws = sb("ws", [P, 4], F32)
        us = sb("us", [P, NC + 2], F32)
        bn = sb("bn", [P, CT, 8, 6], F32)
        mv = sb("mv", [P, CT, 2], F32)
        mean = sb("mean", [P, 2, CT], F32)
        nmean = sb("nmean", [P, 2, CT], F32)
        rstd = sb("rstd", [P, CT], F32)
        stdm = sb("stdm", [P, 2, CT], F32)
        off = sb("off", [P, CT], F32)
        sq = sb("sq", [P, CT], F32)
        spread = sb("spread", [P, CT], F32)
        var = sb("var", [P, CT], F32)
        std0 = sb("std0", [P, CT], F32)
        rs0 = sb("rs0", [P, CT], F32)
        quo = sb("quo", [P, CT], F32)
        std = sb("std", [P, CT], F32)
        rs1 = sb("rs1", [P, CT], F32)
        pooled = sb("pooled", [P, CT], F32)
        ex = sb("ex", [P, 1], F32)
        ex1 = sb("ex1", [P, 1], F32)
        att = sb("att", [P, 1], F32)
        D32 = sb("D32", [P, CI], F32)
        D = sb("D", [P, 2, CI], F16)

        pM = ctx.enter_context(nc.psum_tensor("pM", [P, BANKS, 512], F32))
        pG = ctx.enter_context(nc.psum_tensor("pG", [P, KS, 512], F32))
        pS = ctx.enter_context(nc.psum_tensor("pS", [P, 512], F32))

        W16 = W32[:, :, :, :].bitcast(F16)
        stage = [X[1][:, i, 1:HP - 1, :].rearrange("p r w -> p (r w)")[:, 0:WG] for i in range(2)]

        w_in = [sem(f"w_in{c}") for c in range(CT * 2)]
        small_in = sem("small_in")
        x_in = [sem(f"x_in{c}") for c in range(CH)]
        stored = [sem(f"stored{c}") for c in range(CH)]
        pads_set = sem("pads_set")
        bias_set = sem("bias_set")
        avg_set = sem("avg_set")
        pool_step = sem("pool_step")
        w_top = sem("w_top")
        w_all = sem("w_all")
        w_scaled = sem("w_scaled")
        w_hi = sem("w_hi")
        w_lo_dve = sem("w_lo_dve")
        w_lo_pool = sem("w_lo_pool")
        pieces_ready = sem("pieces_ready")
        mean_ready = sem("mean_ready")
        spread_ready = sem("spread_ready")
        group_mean = sem("group_mean")
        group_var = sem("group_var")
        logits = sem("logits")
        shift_ready = sem("shift_ready")
        var_ready = sem("var_ready")
        std_ready = sem("std_ready")
        pooled_ready = sem("pooled_ready")
        exp_ready = sem("exp_ready")
        att_ready = sem("att_ready")
        centred = sem("centred")
        normed = sem("normed")
        mixed = sem("mixed")
        taps_taken = sem("taps_taken")
        comp_ready = sem("comp_ready")
        hi_done = sem("hi_done")
        lo_done = sem("lo_done")
        group_done = sem("group_done")
        restored = sem("restored")
        dve_took = sem("dve_took")
        act_took = sem("act_took")
        rows_added = sem("rows_added")
        row0_added = sem("row0_added")
        dve_step = sem("dve_step")

        def rows(b, chunk, i):
            r = CR * chunk + i
            return [X[b][:, c, r:r + M * (TR - 1) + 1:M, :] for c in range(CT)]

        def out_rows(b, chunk, o, r):
            q = CR * chunk + 1 + r
            return X[b][:, o, q:q + M * (TR - 1) + 1:M, :]

        def tiled(ap):
            return [ap[:, c * U:(c + 1) * U].rearrange("p (t w) -> p t w", w=W) for c in range(CT)]

        def tile_rows(ap):
            return ap.rearrange("p (t w) -> p t w", w=W)

        def comp_out(j, part, c):
            return Vs[:, j, part, c, 1:1 + TR * VW].rearrange("p (t w) -> p t w", w=VW)[:, :, 0:W]

        def comp_in(j, part, c, kx):
            return Vs[:, j, part, c, kx:kx + TR * VW].rearrange("p (t w) -> p t w", w=VW)[:, :, 0:W]

        def u_flat(j, part, c):
            return Us[:, j, part, c].rearrange("p o k n -> p o (k n)")

        def halves(ap):
            return ap[:, 0:CT * TAPS].rearrange("p (o n) -> p o n", o=CT)

        block = ctx.enter_context(nc.Block())

        @block.sync
        def _(sp):
            def load(n, b, chunk):
                src = x_dram[n] if isinstance(n, int) else x_dram[bass.ds(n, 1)].rearrange("n p c m -> (n p) c m")
                sp.dma_start(X[b][:, :, 1 + CR * chunk:1 + CR * (chunk + 1), :].rearrange("p c r w -> p c (r w)"),
                             src[:, :, CR * W * chunk:CR * W * (chunk + 1)]).then_inc(x_in[chunk], 16)

            def epoch(e, b, more):
                n = e - 1
                for chunk in range(CH):
                    sp.wait_ge(dve_took, e * len(DVE_TAKES) + len(DVE_TAKES) // 2 * (chunk + 1))
                    dst = out_dram[n] if isinstance(n, int) else out_dram[bass.ds(n, 1)].rearrange("n p c m -> (n p) c m")
                    sp.dma_start(dst[:, :, CR * W * chunk:CR * W * (chunk + 1)],
                                 X[b][:, :, 1 + CR * chunk:1 + CR * (chunk + 1), :].rearrange("p c r w -> p c (r w)")
                                 ).then_inc(stored[chunk], 16)
                    sp.wait_ge(stored[chunk], e * 16)
                    if more:
                        load(e + 1, b, chunk)

            for chunk in range(CH):
                load(0, 0, chunk)
            sp.dma_start(attw[:, :, :], att_w.rearrange("(c p) n -> p c n", p=P)).then_inc(small_in, 16)
            sp.dma_start(attb[:, :], att_b).then_inc(small_in, 16)
            for i in range(CT * 2):
                c, j = i // 2, JT // 2 * (i % 2)
                sp.dma_start(W32[:, c, j:j + JT // 2, :],
                             w[:, c * JT + j:c * JT + j + JT // 2, :]).then_inc(w_in[i], 16)
            sp.wait_ge(w_lo_dve, CT * JT // 2)
            sp.wait_ge(w_lo_pool, CT * JT // 2)
            for chunk in range(CH):
                load(1, 1, chunk)
            with sp.Fori(0, (N - 2) // 2) as i:
                epoch(i * 2 + 1, 0, True)
                epoch(i * 2 + 2, 1, True)
            epoch(N - 1, 0, False)
            epoch(N, 1, False)

        @block.tensor
        def _(pe):
            def group_mean_mm(e):
                pe.wait_ge(mean_ready, e + 1)
                pe.matmul(pS[:, 0:CT], avg[:, :], mv[:, :, 0], start=True, stop=True).then_inc(group_mean, 1)

            def group_var_mm(e):
                pe.wait_ge(spread_ready, e + 1)
                pe.matmul(pS[:, CT:2 * CT], avg[:, :], spread[:, :], start=True, stop=True).then_inc(group_var, 1)

            def logits_mm(e):
                pe.wait_ge(pooled_ready, e + 1)
                for c in range(CT):
                    mm = pe.matmul(pS[:, 2 * CT:2 * CT + 1], attw[:, c, :], pooled[:, c:c + 1],
                                   start=(c == 0), stop=(c == CT - 1))
                mm.then_inc(logits, 1)

            def mix(e, u):
                c, h = MIX_UNITS[u]
                if u == 0:
                    pe.wait_ge(att_ready, e + 1)
                for ky in range(KS):
                    pe.wait_ge(taps_taken, e * TAKES + TAKES + KS * (u - 1) + ky + 1)
                    for a, b in ((0, 0), (0, 1), (1, 0)):
                        for j in range(JT):
                            at = b * WG + (h * KS + ky) * TAPS
                            mm = pe.matmul(pG[CI * j:CI * (j + 1), ky, 0:TAPS], D[:, a, :],
                                           W16[:, c, j, at:at + TAPS], start=(a == 0 and b == 0), stop=(a == 1),
                                           tile_position=(0, CI * j))
                    mm.then_inc(mixed, 1)

            def group(e, k, o):
                chunk, j = k // NC, k % NC
                g = CT * k + o
                if o == 0:
                    v, u = ("V", 0, chunk, j), ("U", 0, CT - 1, j)
                    need = [INDEX[i] + 1 if i in INDEX else INDEX[(i[0], 1) + i[2:]] + 1 - NI
                            for i in ((v, u) if chunk == 0 else (v,))]
                    pe.wait_ge(lo_done, e * NI + max(need))
                before = ((k - 2) % SLOTS, o)
                past = len(ACT_TAKES if before in ACT_TAKES else DVE_TAKES) if k < 2 else 0
                if before in ACT_TAKES:
                    pe.wait_ge(act_took, e * len(ACT_TAKES) - past + ACT_TAKES.index(before) + 1)
                else:
                    pe.wait_ge(dve_took, e * len(DVE_TAKES) - past + DVE_TAKES.index(before) + 1)
                n = 0
                for c in range(CT):
                    for kx in range(KS):
                        for a, b in ((0, 0), (0, 1), (1, 0)):
                            mm = pe.matmul(pM[:, g % BANKS, 0:U].rearrange("p (t w) -> p t w", w=W),
                                           Us[:, j, a, c, o, kx, :], comp_in(j, b, c, kx),
                                           start=(n == 0), stop=(n == 3 * KS * CT - 1))
                            n += 1
                mm.then_inc(group_done, 1)

            def epoch(e, more):
                for k in range(SLOTS):
                    for o in range(CT):
                        group(e, k, o)
                        if more:
                            if (k, o) == (3, 0):
                                group_mean_mm(e)
                            if (k, o) == (3, 1):
                                group_var_mm(e)
                            if (k, o) == (5, 0):
                                logits_mm(e)
                            if (6, 1) <= (k, o) <= (8, 0):
                                mix(e, CT * k + o - 13)

            pe.sem_inc(group_done, GROUPS)
            pe.wait_ge(avg_set, 1)
            group_mean_mm(0)
            group_var_mm(0)
            pe.wait_ge(small_in, 32)
            logits_mm(0)
            pe.wait_ge(w_lo_dve, CT * JT // 2)
            pe.wait_ge(w_lo_pool, CT * JT // 2)
            for u in range(len(MIX_UNITS)):
                mix(0, u)
            pe.wait_ge(pads_set, 1)
            with pe.Fori(0, (N - 2) // 2) as i:
                epoch(i * 2 + 1, True)
                epoch(i * 2 + 2, True)
            epoch(N - 1, True)
            epoch(N, False)

        @block.vector
        def _(dve):
            steps, first = [0], [0]

            def step(e, ins, between=None):
                steps[0] += 1
                ins.then_inc(dve_step, 1)
                if between:
                    between(e)
                dve.wait_ge(dve_step, (e - 1) * STEPS + first[0] + steps[0])

            def buffer_free(e, n):
                m = E_INDEX[n] - EB
                last = E_ITEMS[m] if m >= 0 else E_ITEMS[m + NE] - NI
                dve.wait_ge(lo_done, e * NI + last + 1)
                return E[:, E_INDEX[n] % EB, :]

            def temps_free(e, n):
                dve.wait_ge(comp_ready, e * NE + E_INDEX[n])

            def combine(dst, a, scale, d):
                for c in range(CT):
                    ins = dve.scalar_tensor_tensor(out=dst[c], in0=a[c], scalar=scale, in1=d[c],
                                                   op0=ALU.mult, op1=ALU.add)
                return ins

            def v_single(e, b, n, ahead=0):
                _, _, chunk, j = ITEMS[n]
                i = 0 if j == 0 else 1
                t1 = tiled(T1)
                temps_free(e + ahead, n)
                step(e, combine(t1, rows(b, chunk, i + 2), -(A2 + B2), rows(b, chunk, i + 4)))
                dst = tiled(buffer_free(e + ahead, n))
                combine(dst, rows(b, chunk, i), A2 * B2, t1).then_inc(comp_ready, 1)

            def v_pair(e, b, n):
                _, _, chunk, j = ITEMS[n]
                q2 = B2 if j == 1 else A2
                temps_free(e, n)
                combine(tiled(T1), rows(b, chunk, 2), -q2, rows(b, chunk, 4))
                step(e, combine(tiled(T2), rows(b, chunk, 1), -q2, rows(b, chunk, 3)))
                for m in range(2):
                    dst = buffer_free(e, n + m)
                    dve.scalar_tensor_tensor(out=dst, in0=T2[:, :], scalar=POINT[j + m], in1=T1[:, :],
                                             op0=ALU.mult, op1=ALU.add).then_inc(comp_ready, 1)

            def u_pair(e, n, c):
                j = ITEMS[n][3]
                p = POINT[j]
                t = (T1, T2)[c]
                temps_free(e, n)
                step(e, dve.scalar_tensor_tensor(out=halves(t), in0=G[:, c, :, 2, :], scalar=p * p,
                                                 in1=G[:, c, :, 0, :], op0=ALU.mult, op1=ALU.add))
                for m in range(2):
                    dst = buffer_free(e, n + m)
                    dve.scalar_tensor_tensor(out=halves(dst), in0=G[:, c, :, 1, :], scalar=POINT[j + m],
                                             in1=halves(t), op0=ALU.mult, op1=ALU.add).then_inc(comp_ready, 1)

            def stats(e, b, chunk):
                if not (isinstance(e, int) and e == 0):
                    dve.wait_ge(mean_ready, e)
                dve.wait_ge(x_in[chunk], e * 16 + 16)
                for c in range(CT):
                    for q in range(4):
                        r = 1 + CR * chunk + TR * q
                        ins = dve.bn_stats(bn[:, c, 4 * chunk + q, :],
                                           X[b][:, c, r:r + TR, :].rearrange("p r w -> p (r w)"))
                return ins

            def channel_stats(e):
                for c in range(CT):
                    ins = dve.bn_aggr(mv[:, c, :], bn[:, c].rearrange("p q s -> p (q s)"))
                ins.then_inc(mean_ready, 1)

            def group_shift(e, b):
                dve.wait_ge(group_mean, e + 1)
                dve.tensor_scalar(mean[:, b, :], pS[:, 0:CT], 1.0, None, ALU.mult)
                ins = dve.tensor_scalar(nmean[:, b, :], pS[:, 0:CT], -1.0, None, ALU.mult)
                ins.then_inc(shift_ready, 1)
                dve.wait_ge(shift_ready, e + 1)
                step(e, dve.tensor_tensor(off[:, :], mv[:, :, 0], nmean[:, b, :], ALU.add))
                step(e, dve.tensor_tensor(sq[:, :], off[:, :], off[:, :], ALU.mult))
                dve.tensor_tensor(spread[:, :], sq[:, :], mv[:, :, 1], ALU.add).then_inc(spread_ready, 1)

            def group_variance(e):
                dve.wait_ge(group_var, e + 1)
                dve.tensor_scalar(var[:, :], pS[:, CT:2 * CT], EPS, None, ALU.add).then_inc(var_ready, 1)

            def norm_scale(e, b):
                dve.wait_ge(std_ready, e + 1)
                step(e, dve.reciprocal(rs0[:, :], std0[:, :]))
                step(e, dve.tensor_tensor(quo[:, :], var[:, :], rs0[:, :], ALU.mult))
                step(e, dve.tensor_tensor(std[:, :], quo[:, :], std0[:, :], ALU.add))
                step(e, dve.reciprocal(rs1[:, :], std[:, :]))
                dve.tensor_scalar(stdm[:, b, :], std[:, :], 0.5 / V_SCALE, None, ALU.mult)
                dve.tensor_scalar(rstd[:, :], rs1[:, :], 2.0 * V_SCALE, None, ALU.mult)
                dve.scalar_tensor_tensor(out=pooled[:, :], in0=off[:, :], scalar=2.0, in1=rs1[:, :],
                                         op0=ALU.mult, op1=ALU.mult).then_inc(pooled_ready, 1)

            def attention(e):
                dve.wait_ge(exp_ready, e + 1)
                step(e, dve.tensor_scalar(ex1[:, :], ex[:, :], 1.0, None, ALU.add))
                step(e, dve.reciprocal(att[:, :], ex1[:, :]))
                step(e, dve.tensor_scalar(D32[:, :], sel[:, :], att[:, 0:1], ATT_SCALE, ALU.mult, ALU.mult))
                dve.wait_ge(mixed, e * TAKES)
                step(e, dve.tensor_copy(D[:, 0, :], D32[:, :]))
                dve.tensor_tensor(D[:, 1, :], D32[:, :], D[:, 0, :], ALU.subtract).then_inc(att_ready, 1)

            def take(e, b, k, o, between=None):
                chunk, j = k // NC, k % NC
                g = CT * k + o
                res = pM[:, g % BANKS, 0:U]
                dve.wait_ge(group_done, e * GROUPS + g + 1)
                if j in (0, 5):
                    r = 0 if j == 0 else M - 1
                    if j == 0:
                        dve.wait_ge(restored, e * 6 + (2 if chunk == 0 else 6))
                    else:
                        dve.wait_ge(rows_added, e * len(PAIRS) + PAIRS.index((k - 1, o)) + 1)
                        if o == CT - 1:
                            dve.wait_ge(row0_added, e * len(PAIRS) + PAIRS.index((k - 1, o)) + 1)
                    y = out_rows(b, chunk, o, r)
                    dve.scalar_tensor_tensor(out=y, in0=tile_rows(res), scalar=us[:, j:j + 1], in1=y,
                                             op0=ALU.mult, op1=ALU.add).then_inc(dve_took, 1)
                    return
                dve.wait_ge(act_took, e * len(ACT_TAKES) + ACT_TAKES.index((k - 1, o)) + 1)
                dve.wait_ge(row0_added, e * len(PAIRS) + PAIRS.index((k, o)) + 1 - CT)
                step(e, dve.scalar_tensor_tensor(out=SUM[:, o, :], in0=res, scalar=us[:, j:j + 1],
                                                 in1=DIF[:, o, :], op0=ALU.mult, op1=ALU.add), between)
                dve.scalar_tensor_tensor(out=DIF[:, o, :], in0=res, scalar=us[:, NC + j // 2 - 1:NC + j // 2],
                                         in1=DIF[:, o, :], op0=ALU.mult, op1=ALU.add).then_inc(dve_took, 1)
                if j == 2:
                    dve.wait_ge(restored, e * 6 + (4 if chunk == 0 else 6))
                dve.wait_ge(dve_took, e * len(DVE_TAKES) + DVE_TAKES.index((k, o)) + 1)
                for r in (2, 1, 3):
                    y = out_rows(b, chunk, o, r)
                    src = (DIF if r % 2 else SUM)[:, o, :]
                    ins = dve.scalar_tensor_tensor(out=y, in0=tile_rows(src), scalar=POINT[j - 1] ** r, in1=y,
                                                   op0=ALU.mult, op1=ALU.add)
                ins.then_inc(rows_added, 1)

            def epoch(e, b, more):
                steps[0] = 0
                u_pair(e, INDEX[("U", 0, 0, 3)], 0)
                take(e, b, 0, 0)
                u_pair(e, INDEX[("U", 0, 1, 3)], 1)
                take(e, b, 0, 1)
                v_single(e, b, INDEX[("V", 0, 1, 0)])
                if more:
                    stats(e, 1 - b, 0)
                    stats(e, 1 - b, 1).then_inc(pieces_ready, 1)
                    dve.wait_ge(pieces_ready, e + 1)
                take(e, b, 2, 0, channel_stats if more else None)
                if more:
                    group_shift(e, 1 - b)
                take(e, b, 2, 1)
                if more:
                    group_variance(e)
                v_pair(e, b, INDEX[("V", 0, 1, 1)])
                if more:
                    norm_scale(e, 1 - b)
                v_pair(e, b, INDEX[("V", 0, 1, 3)])
                take(e, b, 4, 0)
                take(e, b, 4, 1)
                if more:
                    attention(e)
                v_single(e, b, INDEX[("V", 0, 1, 5)])
                take(e, b, 5, 0)
                take(e, b, 5, 1)
                if more:
                    dve.wait_ge(normed, e * 4 + 4)
                    v_single(e, 1 - b, INDEX[("V", 1, 0, 0)])
                take(e, b, 6, 0)
                if more:
                    v_pair(e, 1 - b, INDEX[("V", 1, 0, 1)])
                take(e, b, 6, 1)
                if more:
                    dve.wait_ge(taps_taken, (e + 1) * TAKES + TAKES // 2)
                    u_pair(e, INDEX[("U", 1, 0, 1)], 0)
                take(e, b, 8, 0)
                take(e, b, 8, 1)
                if more:
                    dve.wait_ge(taps_taken, (e + 1) * TAKES + TAKES)
                    u_pair(e, INDEX[("U", 1, 1, 1)], 1)
                    v_pair(e, 1 - b, INDEX[("V", 1, 0, 3)])
                take(e, b, 10, 0)
                take(e, b, 10, 1)
                take(e, b, 11, 0)
                if more:
                    v_single(e, 1 - b, INDEX[("V", 0, 0, 5)], ahead=1)
                take(e, b, 11, 1)
                assert steps[0] == STEPS or not more, steps

            def prepare_first():
                stats(0, 0, 1).then_inc(pieces_ready, 1)
                dve.wait_ge(pieces_ready, 1)
                channel_stats(0)
                group_shift(0, 0)
                group_variance(0)
                norm_scale(0, 0)

            def prepare_first_components():
                dve.wait_ge(avg_set, 1)
                attention(0)
                dve.wait_ge(normed, 4)
                v_single(0, 0, INDEX[("V", 1, 0, 0)])
                v_pair(0, 0, INDEX[("V", 1, 0, 1)])
                dve.wait_ge(taps_taken, 2 * TAKES)
                for c in range(CT):
                    u_pair(0, INDEX[("U", 1, c, 1)], c)
                v_pair(0, 0, INDEX[("V", 1, 0, 3)])
                v_single(0, 0, INDEX[("V", 0, 0, 5)], ahead=1)

            STEPS = 30
            first[0] = STEPS
            dve.sem_inc(dve_took, len(DVE_TAKES))
            dve.sem_inc(comp_ready, E_INDEX[FIRST_NEXT])
            dve.sem_inc(rows_added, len(PAIRS))
            for b in range(2):
                dve.memset(X[b][:, :, 0:1, :], 0.0)
                dve.memset(X[b][:, :, HP - 1:HP, :], 0.0)
            dve.memset(Vs[:, :, :, :, 0:VW * TR + 1:VW].rearrange("p j s c m -> p (j s c) m"), 0.0).then_inc(pads_set, 1)
            dve.wait_ge(pads_set, 1)
            stats(0, 0, 0)
            prepare_first()
            for i in range(CT * JT):
                if i % 2 == 0:
                    dve.wait_ge(w_in[i // 2], 16)
                ins = dve.tensor_reduce(wmax[:, i:i + 1], W32[:, i // JT, i % JT, :], AX.X, ALU.max,
                                        apply_absolute_value=True)
            step(0, ins)
            dve.tensor_reduce(wtop[:, :], wmax[:, :], AX.X, ALU.max).then_inc(w_top, 1)
            dve.wait_ge(w_all, 1)
            step(0, dve.tensor_scalar(ws[:, 0:1], wall[:, :], 2.0 ** -100, None, ALU.max))
            step(0, dve.reciprocal(ws[:, 1:2], ws[:, 0:1]))
            step(0, dve.tensor_scalar(ws[:, 2:3], ws[:, 1:2], W_TOP, None, ALU.mult))
            step(0, dve.tensor_scalar(ws[:, 2:3].bitcast(I32), ws[:, 2:3].bitcast(I32), 0x7F800000, None,
                                      ALU.bitwise_and))
            step(0, dve.reciprocal(ws[:, 3:4], ws[:, 2:3]))
            for j in range(NC):
                dve.tensor_scalar(us[:, j:j + 1], ws[:, 3:4], UNSCALE / F[j], None, ALU.mult)
            for j in (2, 4):
                dve.tensor_scalar(us[:, NC + j // 2 - 1:NC + j // 2], ws[:, 3:4], -UNSCALE / F[j], None, ALU.mult)

            def w_lo(i):
                dve.wait_ge(w_hi, i + 1)
                dve.tensor_tensor(W16[:, i // JT, i % JT, WG:2 * WG], stage[i % 2],
                                  W16[:, i // JT, i % JT, 0:WG], ALU.subtract).then_inc(w_lo_dve, 1)

            for i in range(CT * JT):
                if i >= 2 and i % 2 == 1:
                    dve.wait_ge(w_lo_pool, i // 2)
                if i >= 2 and i % 2 == 0:
                    dve.wait_ge(w_lo_dve, i // 2)
                dve.tensor_scalar(stage[i % 2], W32[:, i // JT, i % JT, :], ws[:, 2:3], None,
                                  ALU.mult).then_inc(w_scaled, 1)
                if i % 2 == 1:
                    w_lo(i - 1)
            prepare_first_components()
            first[0] = steps[0]
            with dve.Fori(0, (N - 2) // 2) as i:
                epoch(i * 2 + 1, 0, True)
                epoch(i * 2 + 2, 1, True)
            epoch(N - 1, 0, True)
            epoch(N, 1, False)

        @block.scalar
        def _(act):
            def hi(e, n):
                kind, nxt, c, j = ITEMS[n]
                if n == 0:
                    act.wait_ge(group_done, e * GROUPS)
                elif kind == "V" and nxt == 0:
                    act.wait_ge(group_done, e * GROUPS + CT * (j + 1))
                elif nxt == 1:
                    act.wait_ge(group_done, e * GROUPS + CT * (NC + j + 1))
                if kind == "U" and j == 0:
                    act.wait_ge(taps_taken, e * TAKES + TAKES + KS * CT * (c + 1))
                if buffered(ITEMS[n]):
                    act.wait_ge(comp_ready, e * NE + E_INDEX[n] + 1)
                if kind == "V":
                    for t in range(CT):
                        ins = act.copy(comp_out(j, 0, t), tile_rows(E[:, E_INDEX[n] % EB, t * U:(t + 1) * U]))
                else:
                    src = halves(E[:, E_INDEX[n] % EB, :]) if buffered(ITEMS[n]) else G[:, c, :, 0 if j == 0 else 2, :]
                    ins = act.copy(u_flat(j, 0, c), src)
                ins.then_inc(hi_done, 1)

            def take(e, k, o):
                g = CT * k + o
                act.wait_ge(group_done, e * GROUPS + g + 1)
                act.wait_ge(rows_added, e * len(PAIRS) + PAIRS.index((k + 1, o)) + 1 - CT)
                act.activation(DIF[:, o, :], pM[:, g % BANKS, 0:U], ACT.Identity,
                               scale=us[:, k % NC:k % NC + 1]).then_inc(act_took, 1)

            def take_taps(e, u):
                c, h = MIX_UNITS[u]
                if u == 0:
                    act.wait_ge(lo_done, e * NI + INDEX[("U", 0, 1, 4)] + 1)
                for ky in range(KS):
                    act.wait_ge(mixed, e * TAKES + KS * u + ky + 1)
                    act.mul(G[:, c, h, ky, :], pG[:, ky, 0:TAPS], MIX_SCALE).then_inc(taps_taken, 1)

            def restore(e, b, n, first, last):
                act.wait_ge(comp_ready, e * NE + E_INDEX[n] + 1)
                for c in range(CT):
                    y = X[b][:, c, first:last, :]
                    act.activation(y, y, ACT.Identity, bias=mean[:, b, c:c + 1],
                                   scale=stdm[:, b, c:c + 1]).then_inc(restored, 1)

            def centre(e, b, chunk):
                act.wait_ge(shift_ready, e + 1)
                for c in range(CT):
                    y = X[b][:, c, 1 + CR * chunk:1 + CR * (chunk + 1), :]
                    act.activation(y, y, ACT.Identity, bias=nmean[:, b, c:c + 1]).then_inc(centred, 1)

            def norm(e, b, chunk):
                act.wait_ge(pooled_ready, e + 1)
                act.wait_ge(centred, e * 4 + CT * (chunk + 1))
                for c in range(CT):
                    y = X[b][:, c, 1 + CR * chunk:1 + CR * (chunk + 1), :]
                    act.activation(y, y, ACT.Copy, scale=rstd[:, c:c + 1]).then_inc(normed, 1)

            def root(e):
                act.wait_ge(var_ready, e + 1)
                act.activation(std0[:, :], var[:, :], ACT.Sqrt).then_inc(std_ready, 1)

            def exponential(e):
                act.wait_ge(logits, e + 1)
                act.activation(ex[:, :], pS[:, 2 * CT:2 * CT + 1], ACT.Exp, bias=nattb[:, 0:1],
                               scale=-1.0).then_inc(exp_ready, 1)

            def restore_chunk_0(e, b):
                restore(e, b, INDEX[("V", 0, 0, 5)], 1, CR)

            def epoch(e, b, more):
                hi(e, INDEX[("V", 0, 0, 5)])
                for c in range(CT):
                    for j in (3, 4):
                        hi(e, INDEX[("U", 0, c, j)])
                for c in range(CT):
                    hi(e, INDEX[("U", 0, c, 5)])
                hi(e, INDEX[("V", 0, 1, 0)])
                restore(e, b, INDEX[("V", 0, 1, 0)], CR, CR + 1)
                take(e, 1, 0)
                take(e, 1, 1)
                take(e, 3, 0)
                if more:
                    centre(e, 1 - b, 0)
                take(e, 3, 1)
                if more:
                    root(e)
                hi(e, INDEX[("V", 0, 1, 1)])
                hi(e, INDEX[("V", 0, 1, 2)])
                if more:
                    centre(e, 1 - b, 1)
                hi(e, INDEX[("V", 0, 1, 3)])
                hi(e, INDEX[("V", 0, 1, 4)])
                if more:
                    exponential(e)
                    norm(e, 1 - b, 0)
                    norm(e, 1 - b, 1)
                restore(e, b, INDEX[("V", 0, 1, 5)], CR + 1, H + 1)
                if more:
                    take_taps(e, 0)
                hi(e, INDEX[("V", 0, 1, 5)])
                if more:
                    take_taps(e, 1)
                    hi(e, INDEX[("V", 1, 0, 0)])
                take(e, 7, 0)
                if more:
                    take_taps(e, 2)
                take(e, 7, 1)
                if more:
                    take_taps(e, 3)
                    for c in range(CT):
                        hi(e, INDEX[("U", 1, c, 0)])
                    for j in (1, 2):
                        hi(e, INDEX[("V", 1, 0, j)])
                    for c in range(CT):
                        for j in (1, 2):
                            hi(e, INDEX[("U", 1, c, j)])
                take(e, 9, 0)
                take(e, 9, 1)
                if more:
                    for j in (3, 4):
                        hi(e, INDEX[("V", 1, 0, j)])
                    restore_chunk_0(e + 1, 1 - b)

            act.sem_inc(act_took, len(ACT_TAKES))
            act.sem_inc(hi_done, FIRST_NEXT)
            act.sem_inc(restored, 6)
            act.sem_inc(taps_taken, TAKES)
            act.wait_ge(small_in, 32)
            act.mul(nattb[:, :], attb[:, :], -1.0).then_inc(bias_set, 1)
            centre(0, 0, 0)
            root(0)
            centre(0, 0, 1)
            act.wait_ge(bias_set, 1)
            exponential(0)
            for chunk in range(CH):
                norm(0, 0, chunk)
            for i in range(CT * JT):
                act.wait_ge(w_scaled, i + 1)
                act.copy(W16[:, i // JT, i % JT, 0:WG], stage[i % 2]).then_inc(w_hi, 1)
            for u in range(len(MIX_UNITS)):
                take_taps(0, u)
            for n in range(FIRST_NEXT, NI):
                hi(0, n)
            restore_chunk_0(1, 0)
            with act.Fori(0, (N - 2) // 2) as i:
                epoch(i * 2 + 1, 0, True)
                epoch(i * 2 + 2, 1, True)
            epoch(N - 1, 0, True)
            epoch(N, 1, False)

        @block.gpsimd
        def _(pool):
            def lo(e, n):
                kind, nxt, c, j = ITEMS[n]
                pool.wait_ge(hi_done, e * NI + n + 1)
                if kind == "V":
                    for t in range(CT):
                        ins = pool.tensor_tensor(comp_out(j, 1, t), tile_rows(E[:, E_INDEX[n] % EB, t * U:(t + 1) * U]),
                                                 comp_out(j, 0, t), ALU.subtract)
                else:
                    src = halves(E[:, E_INDEX[n] % EB, :]) if buffered(ITEMS[n]) else G[:, c, :, 0 if j == 0 else 2, :]
                    ins = pool.tensor_tensor(u_flat(j, 1, c), src, u_flat(j, 0, c), ALU.subtract)
                ins.then_inc(lo_done, 1)

            def add(e, b, k, o):
                pool.wait_ge(dve_took, e * len(DVE_TAKES) + DVE_TAKES.index((k, o)) + 1)
                if k % NC == 4:
                    pool.wait_ge(row0_added, e * len(PAIRS) + PAIRS.index((k, o)) + 1 - CT)
                y = out_rows(b, k // NC, o, 0)
                pool.tensor_tensor(y, y, tile_rows(SUM[:, o, :]), ALU.add).then_inc(row0_added, 1)

            def epoch(e, b, more):
                def items(first, last):
                    for n in range(INDEX[first], INDEX[last] + 1):
                        lo(e, n)

                items(("V", 0, 0, 5), ("V", 0, 1, 0))
                add(e, b, 2, 0)
                add(e, b, 2, 1)
                items(("V", 0, 1, 1), ("V", 0, 1, 3))
                add(e, b, 4, 0)
                items(("V", 0, 1, 4), ("V", 0, 1, 4))
                add(e, b, 4, 1)
                items(("V", 0, 1, 5), ("V", 0, 1, 5))
                if more:
                    items(("V", 1, 0, 0), ("V", 1, 0, 1))
                add(e, b, 8, 0)
                if more:
                    items(("V", 1, 0, 2), ("V", 1, 0, 2))
                add(e, b, 8, 1)
                if more:
                    items(("U", 1, 0, 1), ("V", 1, 0, 3))
                add(e, b, 10, 0)
                if more:
                    items(("V", 1, 0, 4), ("V", 1, 0, 4))
                add(e, b, 10, 1)

            pool.sem_inc(lo_done, FIRST_NEXT)
            pool.sem_inc(row0_added, len(PAIRS))
            pool.memset(sel[:, :], 0.0).then_inc(pool_step, 1)
            pool.wait_ge(pool_step, 1)
            for k in range(K):
                pool.affine_select(out=sel[:, :], in_=sel[:, :], compare_op=ALU.not_equal, fill=1.0, base=-CI * k,
                                   pattern=[[-1, CI]], channel_multiplier=1).then_inc(pool_step, 1)
                pool.wait_ge(pool_step, k + 2)
            blocks = avg[:, :].rearrange("p (g j) -> p g j", j=GS)
            pool.memset(avg[:, :], 1.0 / GS).then_inc(pool_step, 1)
            pool.wait_ge(pool_step, K + 2)
            pool.affine_select(out=blocks, in_=blocks, compare_op=ALU.is_ge, fill=0.0, base=0,
                               pattern=[[-GS, P // GS], [0, GS]], channel_multiplier=1).then_inc(pool_step, 1)
            pool.wait_ge(pool_step, K + 3)
            pool.affine_select(out=blocks, in_=blocks, compare_op=ALU.is_ge, fill=0.0, base=GS - 1,
                               pattern=[[GS, P // GS], [0, GS]], channel_multiplier=-1).then_inc(avg_set, 1)
            pool.wait_ge(w_top, 1)
            pool.partition_all_reduce(wall[:, :], wtop[:, :], P, bass.bass_isa.ReduceOp.max).then_inc(w_all, 1)
            for i in range(1, CT * JT, 2):
                pool.wait_ge(w_hi, i + 1)
                pool.tensor_tensor(W16[:, i // JT, i % JT, WG:2 * WG], stage[1],
                                   W16[:, i // JT, i % JT, 0:WG], ALU.subtract).then_inc(w_lo_pool, 1)
            for n in range(FIRST_NEXT, NI):
                lo(0, n)
            with pool.Fori(0, (N - 2) // 2) as i:
                epoch(i * 2 + 1, 0, True)
                epoch(i * 2 + 2, 1, True)
            epoch(N - 1, 0, True)
            epoch(N, 1, False)


def kernel(x, L0_conv_weight, L0_conv_att_w, L0_conv_att_b):
    import numpy as np
    import concourse.bacc as bacc
    from concourse.bass_utils import run_bass_kernel_spmd

    nc = bacc.Bacc("TRN2", target_bir_lowering=False, num_devices=1, dynamic_dma_scratch_size=16)
    w = np.ascontiguousarray(L0_conv_weight).reshape(K, CT, P, CT, JT, CI, KS, KS)
    w = np.ascontiguousarray(w.transpose(0, 5, 3, 4, 1, 6, 7, 2)).reshape(P, CT * JT, WG)
    arrays = {
        "x_dram": np.ascontiguousarray(x),
        "w_dram": w,
        "attw_dram": np.repeat(np.ascontiguousarray(L0_conv_att_w).T, CI, axis=1),
        "attb_dram": np.repeat(np.ascontiguousarray(L0_conv_att_b), CI).reshape(P, 1),
    }
    args = [nc.dram_tensor(n, a.shape, F32, kind="ExternalInput").ap() for n, a in arrays.items()]
    args.append(nc.dram_tensor("out_dram", (N, C, H, W), F32, kind="ExternalOutput").ap())
    conv_kernel(nc, *args)
    return run_bass_kernel_spmd(nc, [arrays], core_ids=[0]).results[0]["out_dram"]
```

```python
from contextlib import ExitStack

import concourse.bass as bass
from concourse import mybir

P = 128
N, C, H, W = 16, 256, 56, 56
K, KS = 4, 3
CT = C // P
M = 4
NC = M + KS - 1
CH = 2
CR = H // CH
TR = CR // M
U = TR * W
HP = H + 2
VW = W + 1
VROW = TR * VW + 3
GS = 8
CI = 32
JT = P // CI
TAPS = KS * P
WG = CT * KS * TAPS
EPS = 1e-5

PA, PB = 0.75, 1.5
A2, B2 = PA * PA, PB * PB
F_0, F_A, F_B = A2 * B2, 2 * A2 * (A2 - B2), 2 * B2 * (B2 - A2)
POINT = [0.0, PA, -PA, PB, -PB, None]

V_SCALE = 64.0
ATT_SCALE = 2048.0
W_TOP = 2.0 ** 14
MIX_SCALE = 2.0 ** -14
F = [F_0, F_A, F_A, F_B, F_B, 1.0]
UNSCALE = 1.0 / (V_SCALE * ATT_SCALE * MIX_SCALE)

ALU = mybir.AluOpType
ACT = mybir.ActivationFunctionType
AX = mybir.AxisListType
F32 = mybir.dt.float32
F16 = mybir.dt.float16
I32 = mybir.dt.int32

SLOTS = CH * NC
GROUPS = SLOTS * CT
BANKS = 4
EB = 4

ITEMS = ([("V", 0, 0, 5)] + [("U", 0, c, j) for c in range(CT) for j in (3, 4)]
         + [("U", 0, c, 5) for c in range(CT)]
         + [("V", 0, 1, j) for j in range(NC)]
         + [("V", 1, 0, 0)] + [("U", 1, c, 0) for c in range(CT)]
         + [("V", 1, 0, 1), ("V", 1, 0, 2)]
         + [("U", 1, c, j) for c in range(CT) for j in (1, 2)]
         + [("V", 1, 0, 3), ("V", 1, 0, 4)])
NI = len(ITEMS)
INDEX = {it: n for n, it in enumerate(ITEMS)}


def buffered(it):
    return it[0] == "V" or it[3] in (1, 2, 3, 4)


E_ITEMS = [n for n, it in enumerate(ITEMS) if buffered(it)]
NE = len(E_ITEMS)
E_INDEX = {n: m for m, n in enumerate(E_ITEMS)}
FIRST_NEXT = INDEX[("V", 1, 0, 0)]
DVE_TAKES = [(k, o) for k in range(SLOTS) if k % NC in (0, 2, 4, 5) for o in range(CT)]
ACT_TAKES = [(k, o) for k in range(SLOTS) if k % NC in (1, 3) for o in range(CT)]
PAIRS = [(k, o) for k in range(SLOTS) if k % NC in (2, 4) for o in range(CT)]
PART = 512
FULL, REST = divmod(WG, PART)
assert CT == 2 and CT * REST == PART
MIX_BANKS = 3
TAKES = CT * FULL + 1
TILE_TAKES = (FULL + 1, TAKES)
MIX_UNITS = TAKES // MIX_BANKS


def conv_kernel(nc, x, w, att_w, att_b, out):
    x_dram = x.rearrange("n (c p) h w -> n p c (h w)", p=P)
    out_dram = out.rearrange("n (c p) h w -> n p c (h w)", p=P)

    with ExitStack() as ctx:
        def sb(name, shape, dt):
            return ctx.enter_context(nc.sbuf_tensor(name, shape, dt))

        def sem(name):
            return ctx.enter_context(nc.semaphore(name))

        X = [sb(f"X{b}", [P, CT, HP, W], F32) for b in range(2)]
        Vs = sb("Vs", [P, NC, 2, CT, VROW], F16)
        Us = sb("Us", [P, NC, 2, CT, CT, KS, P], F16)
        G = sb("G", [P, CT, CT, KS, TAPS], F32)
        W32 = sb("W32", [P, CT, JT, WG], F32)
        E = sb("E", [P, EB, CT * U], F32)
        T1 = sb("T1", [P, CT * U], F32)
        T2 = sb("T2", [P, CT * U], F32)
        SUM = sb("SUM", [P, CT, U], F32)
        DIF = sb("DIF", [P, CT, U], F32)
        avg = sb("avg", [P, P], F32)
        sel = sb("sel", [P, CI], F32)
        attw = sb("attw", [P, CT, P], F32)
        attb = sb("attb", [P, 1], F32)
        nattb = sb("nattb", [P, 1], F32)
        wmax = sb("wmax", [P, CT * JT], F32)
        wtop = sb("wtop", [P, 1], F32)
        wall = sb("wall", [P, 1], F32)
        ws = sb("ws", [P, 4], F32)
        us = sb("us", [P, NC + 2], F32)
        bn = sb("bn", [P, CT, 8, 6], F32)
        mv = sb("mv", [P, CT, 2], F32)
        mean = sb("mean", [P, 2, CT], F32)
        nmean = sb("nmean", [P, 2, CT], F32)
        rstd = sb("rstd", [P, CT], F32)
        stdm = sb("stdm", [P, 2, CT], F32)
        off = sb("off", [P, CT], F32)
        sq = sb("sq", [P, CT], F32)
        spread = sb("spread", [P, CT], F32)
        var = sb("var", [P, CT], F32)
        std0 = sb("std0", [P, CT], F32)
        rs0 = sb("rs0", [P, CT], F32)
        quo = sb("quo", [P, CT], F32)
        std = sb("std", [P, CT], F32)
        rs1 = sb("rs1", [P, CT], F32)
        pooled = sb("pooled", [P, CT], F32)
        ex = sb("ex", [P, 1], F32)
        ex1 = sb("ex1", [P, 1], F32)
        att = sb("att", [P, 1], F32)
        D32 = sb("D32", [P, CI], F32)
        D = sb("D", [P, 2, CI], F16)

        pM = ctx.enter_context(nc.psum_tensor("pM", [P, BANKS, 512], F32))
        pG = ctx.enter_context(nc.psum_tensor("pG", [P, MIX_BANKS, PART], F32))
        pS = ctx.enter_context(nc.psum_tensor("pS", [P, 512], F32))

        W16 = W32[:, :, :, :].bitcast(F16)
        w_piece = ([W32[:, i // JT, i % JT, :] for i in range(2, CT * JT)]
                   + [X[1][:, i, 1:HP - 1, :].rearrange("p r w -> p (r w)")[:, 0:WG] for i in range(2)])

        w_in = [sem(f"w_in{i}") for i in range(CT * JT)]
        small_in = sem("small_in")
        x_in = [[sem(f"x_in{chunk}{c}") for c in range(CT)] for chunk in range(CH)]
        stored = [[sem(f"stored{chunk}{c}") for c in range(CT)] for chunk in range(CH)]
        pads_set = sem("pads_set")
        bias_set = sem("bias_set")
        avg_set = sem("avg_set")
        pool_step = sem("pool_step")
        w_top = sem("w_top")
        w_all = sem("w_all")
        scale_set = sem("scale_set")
        w_hi = sem("w_hi")
        w_lo = sem("w_lo")
        pieces_ready = sem("pieces_ready")
        mean_ready = sem("mean_ready")
        spread_ready = sem("spread_ready")
        group_mean = sem("group_mean")
        group_var = sem("group_var")
        logits = sem("logits")
        shift_ready = sem("shift_ready")
        var_ready = sem("var_ready")
        std_ready = sem("std_ready")
        pooled_ready = sem("pooled_ready")
        exp_ready = sem("exp_ready")
        att_ready = sem("att_ready")
        centred = sem("centred")
        normed = sem("normed")
        mixed = sem("mixed")
        taps_taken = sem("taps_taken")
        comp_ready = sem("comp_ready")
        hi_done = sem("hi_done")
        lo_done = sem("lo_done")
        group_done = sem("group_done")
        restored = sem("restored")
        dve_took = sem("dve_took")
        act_took = sem("act_took")
        rows_added = sem("rows_added")
        row0_added = sem("row0_added")
        dve_step = sem("dve_step")

        def rows(b, chunk, i):
            r = CR * chunk + i
            return [X[b][:, c, r:r + M * (TR - 1) + 1:M, :] for c in range(CT)]

        def out_rows(b, chunk, o, r):
            q = CR * chunk + 1 + r
            return X[b][:, o, q:q + M * (TR - 1) + 1:M, :]

        def tiled(ap):
            return [ap[:, c * U:(c + 1) * U].rearrange("p (t w) -> p t w", w=W) for c in range(CT)]

        def tile_rows(ap):
            return ap.rearrange("p (t w) -> p t w", w=W)

        def comp_out(j, part, c):
            return Vs[:, j, part, c, 1:1 + TR * VW].rearrange("p (t w) -> p t w", w=VW)[:, :, 0:W]

        def comp_in(j, part, c, kx):
            return Vs[:, j, part, c, kx:kx + TR * VW].rearrange("p (t w) -> p t w", w=VW)[:, :, 0:W]

        def u_flat(j, part, c):
            return Us[:, j, part, c].rearrange("p o k n -> p o (k n)")

        def mix_part(ap, m):
            if m == FULL:
                return ap[:, :, FULL * PART:WG]
            c, at = (0, m) if m < FULL else (1, m - FULL - 1)
            return ap[:, c, PART * at:PART * (at + 1)]

        def halves(ap):
            return ap[:, 0:CT * TAPS].rearrange("p (o n) -> p o n", o=CT)

        block = ctx.enter_context(nc.Block())

        @block.sync
        def _(sp):
            def sample(ap, n):
                return ap[n] if isinstance(n, int) else ap[bass.ds(n, 1)].rearrange("n p c m -> (n p) c m")

            def held(b, chunk, c):
                return X[b][:, c, 1 + CR * chunk:1 + CR * (chunk + 1), :].rearrange("p r w -> p (r w)")

            def load(n, b, chunk, c):
                sp.dma_start(held(b, chunk, c),
                             sample(x_dram, n)[:, c, CR * W * chunk:CR * W * (chunk + 1)]).then_inc(x_in[chunk][c], 16)

            def epoch(e, b, more):
                for chunk in range(CH):
                    for o in range(CT):
                        sp.wait_ge(dve_took, e * len(DVE_TAKES) + len(DVE_TAKES) // CH * (chunk + 1) + o + 1 - CT)
                        sp.dma_start(sample(out_dram, e - 1)[:, o, CR * W * chunk:CR * W * (chunk + 1)],
                                     held(b, chunk, o)).then_inc(stored[chunk][o], 16)
                    if more:
                        for c in range(CT):
                            sp.wait_ge(stored[chunk][c], e * 16)
                            load(e + 1, b, chunk, c)

            for chunk in range(CH):
                for c in range(CT):
                    load(0, 0, chunk, c)
            sp.dma_start(attw[:, :, :], att_w.rearrange("(c p) n -> p c n", p=P)).then_inc(small_in, 16)
            sp.dma_start(attb[:, :], att_b).then_inc(small_in, 16)
            for i in range(CT * JT):
                sp.dma_start(w_piece[i], w[:, i, :]).then_inc(w_in[i], 16)
            sp.wait_ge(w_lo, CT * JT)
            for chunk in range(CH):
                for c in range(CT):
                    load(1, 1, chunk, c)
            with sp.Fori(0, (N - 2) // 2) as i:
                epoch(i * 2 + 1, 0, True)
                epoch(i * 2 + 2, 1, True)
            epoch(N - 1, 0, False)
            epoch(N, 1, False)
            for chunk in range(CH):
                for c in range(CT):
                    sp.wait_ge(stored[chunk][c], N * 16)

        @block.tensor
        def _(pe):
            def group_mean_mm(e):
                pe.wait_ge(mean_ready, e + 1)
                pe.matmul(pS[:, 0:CT], avg[:, :], mv[:, :, 0], start=True, stop=True).then_inc(group_mean, 1)

            def group_var_mm(e):
                pe.wait_ge(spread_ready, e + 1)
                pe.matmul(pS[:, CT:2 * CT], avg[:, :], spread[:, :], start=True, stop=True).then_inc(group_var, 1)

            def logits_mm(e):
                pe.wait_ge(pooled_ready, e + 1)
                for c in range(CT):
                    mm = pe.matmul(pS[:, 2 * CT:2 * CT + 1], attw[:, c, :], pooled[:, c:c + 1],
                                   start=(c == 0), stop=(c == CT - 1))
                mm.then_inc(logits, 1)

            def mix(e, u):
                if u == 0:
                    pe.wait_ge(att_ready, e + 1)
                for m in range(MIX_BANKS * u, MIX_BANKS * (u + 1)):
                    pe.wait_ge(taps_taken, e * TAKES + TAKES + m - MIX_BANKS + 1)
                    for a, b in ((0, 0), (0, 1), (1, 0)):
                        for j in range(JT):
                            dst = pG[CI * j:CI * (j + 1), m % MIX_BANKS, :]
                            if m == FULL:
                                dst = dst.rearrange("p (c n) -> p c n", c=CT)
                            mm = pe.matmul(dst, D[:, a, :], mix_part(W16[:, :, j, b * WG:(b + 1) * WG], m),
                                           start=(a == 0 and b == 0), stop=(a == 1), tile_position=(0, CI * j))
                    mm.then_inc(mixed, 1)

            def group(e, k, o):
                chunk, j = k // NC, k % NC
                g = CT * k + o
                if o == 0:
                    v, u = ("V", 0, chunk, j), ("U", 0, CT - 1, j)
                    need = [INDEX[i] + 1 if i in INDEX else INDEX[(i[0], 1) + i[2:]] + 1 - NI
                            for i in ((v, u) if chunk == 0 else (v,))]
                    pe.wait_ge(lo_done, e * NI + max(need))
                before = ((k - 2) % SLOTS, o)
                past = len(ACT_TAKES if before in ACT_TAKES else DVE_TAKES) if k < 2 else 0
                if before in ACT_TAKES:
                    pe.wait_ge(act_took, e * len(ACT_TAKES) - past + ACT_TAKES.index(before) + 1)
                else:
                    pe.wait_ge(dve_took, e * len(DVE_TAKES) - past + DVE_TAKES.index(before) + 1)
                n = 0
                for c in range(CT):
                    for kx in range(KS):
                        for a, b in ((0, 0), (0, 1), (1, 0)):
                            mm = pe.matmul(pM[:, g % BANKS, 0:U].rearrange("p (t w) -> p t w", w=W),
                                           Us[:, j, a, c, o, kx, :], comp_in(j, b, c, kx),
                                           start=(n == 0), stop=(n == 3 * KS * CT - 1))
                            n += 1
                mm.then_inc(group_done, 1)

            def epoch(e, more):
                for k in range(SLOTS):
                    for o in range(CT):
                        group(e, k, o)
                        if more:
                            if (k, o) == (3, 0):
                                group_mean_mm(e)
                            if (k, o) == (3, 1):
                                group_var_mm(e)
                            if (k, o) == (5, 0):
                                logits_mm(e)
                            if (6, 1) <= (k, o) <= (7, 1):
                                mix(e, CT * k + o - 13)

            def keep_clock(n):
                for _ in range(n):
                    pe.matmul(pS[:, P:P + TAPS], W16[:, 0, 0, 0:P], W16[:, 0, 0, 0:TAPS], start=True, stop=True)

            pe.sem_inc(group_done, GROUPS)
            pe.wait_ge(avg_set, 1)
            group_mean_mm(0)
            group_var_mm(0)
            pe.wait_ge(small_in, 32)
            logits_mm(0)
            for u in range(MIX_UNITS):
                pe.wait_ge(w_lo, JT if MIX_BANKS * (u + 1) <= FULL else CT * JT)
                mix(0, u)
                if u == 0:
                    keep_clock(24)
            keep_clock(16)
            pe.wait_ge(pads_set, 1)
            with pe.Fori(0, (N - 2) // 2) as i:
                epoch(i * 2 + 1, True)
                epoch(i * 2 + 2, True)
            epoch(N - 1, True)
            epoch(N, False)

        @block.vector
        def _(dve):
            steps, first = [0], [0]

            def step(e, ins, between=None):
                steps[0] += 1
                ins.then_inc(dve_step, 1)
                if between:
                    between(e)
                dve.wait_ge(dve_step, (e - 1) * STEPS + first[0] + steps[0])

            def buffer_free(e, n):
                m = E_INDEX[n] - EB
                last = E_ITEMS[m] if m >= 0 else E_ITEMS[m + NE] - NI
                dve.wait_ge(lo_done, e * NI + last + 1)
                return E[:, E_INDEX[n] % EB, :]

            def temps_free(e, n):
                dve.wait_ge(comp_ready, e * NE + E_INDEX[n])

            def combine(dst, a, scale, d):
                for c in range(CT):
                    ins = dve.scalar_tensor_tensor(out=dst[c], in0=a[c], scalar=scale, in1=d[c],
                                                   op0=ALU.mult, op1=ALU.add)
                return ins

            def v_single(e, b, n, ahead=0):
                _, _, chunk, j = ITEMS[n]
                i = 0 if j == 0 else 1
                t1 = tiled(T1)
                temps_free(e + ahead, n)
                step(e, combine(t1, rows(b, chunk, i + 2), -(A2 + B2), rows(b, chunk, i + 4)))
                dst = tiled(buffer_free(e + ahead, n))
                combine(dst, rows(b, chunk, i), A2 * B2, t1).then_inc(comp_ready, 1)

            def v_pair(e, b, n):
                _, _, chunk, j = ITEMS[n]
                q2 = B2 if j == 1 else A2
                temps_free(e, n)
                combine(tiled(T1), rows(b, chunk, 2), -q2, rows(b, chunk, 4))
                step(e, combine(tiled(T2), rows(b, chunk, 1), -q2, rows(b, chunk, 3)))
                for m in range(2):
                    dst = buffer_free(e, n + m)
                    dve.scalar_tensor_tensor(out=dst, in0=T2[:, :], scalar=POINT[j + m], in1=T1[:, :],
                                             op0=ALU.mult, op1=ALU.add).then_inc(comp_ready, 1)

            def u_pair(e, n, c):
                j = ITEMS[n][3]
                p = POINT[j]
                t = (T1, T2)[c]
                temps_free(e, n)
                step(e, dve.scalar_tensor_tensor(out=halves(t), in0=G[:, c, :, 2, :], scalar=p * p,
                                                 in1=G[:, c, :, 0, :], op0=ALU.mult, op1=ALU.add))
                for m in range(2):
                    dst = buffer_free(e, n + m)
                    dve.scalar_tensor_tensor(out=halves(dst), in0=G[:, c, :, 1, :], scalar=POINT[j + m],
                                             in1=halves(t), op0=ALU.mult, op1=ALU.add).then_inc(comp_ready, 1)

            def stats(e, b, chunk):
                if not (isinstance(e, int) and e == 0):
                    dve.wait_ge(mean_ready, e)
                for c in range(CT):
                    dve.wait_ge(x_in[chunk][c], e * 16 + 16)
                    for q in range(4):
                        r = 1 + CR * chunk + TR * q
                        ins = dve.bn_stats(bn[:, c, 4 * chunk + q, :],
                                           X[b][:, c, r:r + TR, :].rearrange("p r w -> p (r w)"))
                return ins

            def channel_stats(e):
                for c in range(CT):
                    ins = dve.bn_aggr(mv[:, c, :], bn[:, c].rearrange("p q s -> p (q s)"))
                ins.then_inc(mean_ready, 1)

            def group_shift(e, b):
                dve.wait_ge(group_mean, e + 1)
                dve.tensor_scalar(mean[:, b, :], pS[:, 0:CT], 1.0, None, ALU.mult)
                ins = dve.tensor_scalar(nmean[:, b, :], pS[:, 0:CT], -1.0, None, ALU.mult)
                ins.then_inc(shift_ready, 1)
                dve.wait_ge(shift_ready, e + 1)
                step(e, dve.tensor_tensor(off[:, :], mv[:, :, 0], nmean[:, b, :], ALU.add))
                step(e, dve.tensor_tensor(sq[:, :], off[:, :], off[:, :], ALU.mult))
                dve.tensor_tensor(spread[:, :], sq[:, :], mv[:, :, 1], ALU.add).then_inc(spread_ready, 1)

            def group_variance(e):
                dve.wait_ge(group_var, e + 1)
                dve.tensor_scalar(var[:, :], pS[:, CT:2 * CT], EPS, None, ALU.add).then_inc(var_ready, 1)

            def norm_scale(e, b):
                dve.wait_ge(std_ready, e + 1)
                step(e, dve.reciprocal(rs0[:, :], std0[:, :]))
                step(e, dve.tensor_tensor(quo[:, :], var[:, :], rs0[:, :], ALU.mult))
                step(e, dve.tensor_tensor(std[:, :], quo[:, :], std0[:, :], ALU.add))
                step(e, dve.reciprocal(rs1[:, :], std[:, :]))
                dve.tensor_scalar(stdm[:, b, :], std[:, :], 0.5 / V_SCALE, None, ALU.mult)
                dve.tensor_scalar(rstd[:, :], rs1[:, :], 2.0 * V_SCALE, None, ALU.mult)
                dve.scalar_tensor_tensor(out=pooled[:, :], in0=off[:, :], scalar=2.0, in1=rs1[:, :],
                                         op0=ALU.mult, op1=ALU.mult).then_inc(pooled_ready, 1)

            def attention(e):
                dve.wait_ge(exp_ready, e + 1)
                step(e, dve.tensor_scalar(ex1[:, :], ex[:, :], 1.0, None, ALU.add))
                step(e, dve.reciprocal(att[:, :], ex1[:, :]))
                step(e, dve.tensor_scalar(D32[:, :], sel[:, :], att[:, 0:1], ATT_SCALE, ALU.mult, ALU.mult))
                dve.wait_ge(mixed, e * TAKES)
                step(e, dve.tensor_copy(D[:, 0, :], D32[:, :]))
                dve.tensor_tensor(D[:, 1, :], D32[:, :], D[:, 0, :], ALU.subtract).then_inc(att_ready, 1)

            def take(e, b, k, o, between=None):
                chunk, j = k // NC, k % NC
                g = CT * k + o
                res = pM[:, g % BANKS, 0:U]
                dve.wait_ge(group_done, e * GROUPS + g + 1)
                if j in (0, 5):
                    r = 0 if j == 0 else M - 1
                    if j == 0:
                        dve.wait_ge(restored, e * 6 + (2 if chunk == 0 else 6))
                    else:
                        dve.wait_ge(rows_added, e * len(PAIRS) + PAIRS.index((k - 1, o)) + 1)
                        dve.wait_ge(row0_added, e * len(PAIRS) + PAIRS.index((k - 1, o)) + 1)
                    y = out_rows(b, chunk, o, r)
                    dve.scalar_tensor_tensor(out=y, in0=tile_rows(res), scalar=us[:, j:j + 1], in1=y,
                                             op0=ALU.mult, op1=ALU.add).then_inc(dve_took, 1)
                    return
                dve.wait_ge(act_took, e * len(ACT_TAKES) + ACT_TAKES.index((k - 1, o)) + 1)
                dve.wait_ge(row0_added, e * len(PAIRS) + PAIRS.index((k, o)) + 1 - CT)
                step(e, dve.scalar_tensor_tensor(out=SUM[:, o, :], in0=res, scalar=us[:, j:j + 1],
                                                 in1=DIF[:, o, :], op0=ALU.mult, op1=ALU.add), between)
                dve.scalar_tensor_tensor(out=DIF[:, o, :], in0=res, scalar=us[:, NC + j // 2 - 1:NC + j // 2],
                                         in1=DIF[:, o, :], op0=ALU.mult, op1=ALU.add).then_inc(dve_took, 1)
                if j == 2:
                    dve.wait_ge(restored, e * 6 + (4 if chunk == 0 else 6))
                dve.wait_ge(dve_took, e * len(DVE_TAKES) + DVE_TAKES.index((k, o)) + 1)
                for r in (2, 1, 3):
                    y = out_rows(b, chunk, o, r)
                    src = (DIF if r % 2 else SUM)[:, o, :]
                    ins = dve.scalar_tensor_tensor(out=y, in0=tile_rows(src), scalar=POINT[j - 1] ** r, in1=y,
                                                   op0=ALU.mult, op1=ALU.add)
                ins.then_inc(rows_added, 1)

            def epoch(e, b, more, ahead):
                steps[0] = 0
                u_pair(e, INDEX[("U", 0, 0, 3)], 0)
                take(e, b, 0, 0)
                u_pair(e, INDEX[("U", 0, 1, 3)], 1)
                take(e, b, 0, 1)
                v_single(e, b, INDEX[("V", 0, 1, 0)])
                if more:
                    stats(e, 1 - b, 1).then_inc(pieces_ready, 1)
                    dve.wait_ge(pieces_ready, e + 1)
                take(e, b, 2, 0, channel_stats if more else None)
                if more:
                    group_shift(e, 1 - b)
                take(e, b, 2, 1)
                if more:
                    group_variance(e)
                v_pair(e, b, INDEX[("V", 0, 1, 1)])
                if more:
                    norm_scale(e, 1 - b)
                v_pair(e, b, INDEX[("V", 0, 1, 3)])
                take(e, b, 4, 0)
                take(e, b, 4, 1)
                if more:
                    attention(e)
                v_single(e, b, INDEX[("V", 0, 1, 5)])
                take(e, b, 5, 0)
                take(e, b, 5, 1)
                if more:
                    dve.wait_ge(normed, e * 4 + 4)
                    v_single(e, 1 - b, INDEX[("V", 1, 0, 0)])
                take(e, b, 6, 0)
                if more:
                    v_pair(e, 1 - b, INDEX[("V", 1, 0, 1)])
                take(e, b, 6, 1)
                if more:
                    dve.wait_ge(taps_taken, (e + 1) * TAKES + TILE_TAKES[0])
                    u_pair(e, INDEX[("U", 1, 0, 1)], 0)
                if ahead:
                    stats(e + 1, b, 0)
                take(e, b, 8, 0)
                take(e, b, 8, 1)
                if more:
                    dve.wait_ge(taps_taken, (e + 1) * TAKES + TILE_TAKES[1])
                    u_pair(e, INDEX[("U", 1, 1, 1)], 1)
                    v_pair(e, 1 - b, INDEX[("V", 1, 0, 3)])
                take(e, b, 10, 0)
                take(e, b, 10, 1)
                take(e, b, 11, 0)
                if more:
                    v_single(e, 1 - b, INDEX[("V", 0, 0, 5)], ahead=1)
                take(e, b, 11, 1)
                assert steps[0] == STEPS or not more, steps

            def w_max(i):
                dve.wait_ge(w_in[i], 16)
                return dve.tensor_reduce(wmax[:, i:i + 1], w_piece[i], AX.X, ALU.max, apply_absolute_value=True)

            STEPS = 30
            first[0] = STEPS
            dve.sem_inc(dve_took, len(DVE_TAKES))
            dve.sem_inc(comp_ready, E_INDEX[FIRST_NEXT])
            dve.sem_inc(rows_added, len(PAIRS))
            for b in range(2):
                dve.memset(X[b][:, :, 0:1, :], 0.0)
                dve.memset(X[b][:, :, HP - 1:HP, :], 0.0)
            dve.memset(Vs[:, :, :, :, 0:VW * TR + 1:VW].rearrange("p j s c m -> p (j s c) m"), 0.0).then_inc(pads_set, 1)
            dve.wait_ge(pads_set, 1)
            stats(0, 0, 0)
            stats(0, 0, 1).then_inc(pieces_ready, 1)
            dve.wait_ge(pieces_ready, 1)
            channel_stats(0)
            w_max(0)
            group_shift(0, 0)
            group_variance(0)
            w_max(1)
            norm_scale(0, 0)
            w_max(2)
            w_max(3)
            dve.wait_ge(avg_set, 1)
            attention(0)
            w_max(4)
            w_max(5)
            w_max(6)
            step(0, w_max(7))
            dve.tensor_reduce(wtop[:, :], wmax[:, :], AX.X, ALU.max).then_inc(w_top, 1)
            dve.wait_ge(w_all, 1)
            step(0, dve.tensor_scalar(ws[:, 0:1], wall[:, :], 2.0 ** -100, None, ALU.max))
            step(0, dve.reciprocal(ws[:, 1:2], ws[:, 0:1]))
            step(0, dve.tensor_scalar(ws[:, 2:3], ws[:, 1:2], W_TOP, None, ALU.mult))
            step(0, dve.tensor_scalar(ws[:, 2:3].bitcast(I32), ws[:, 2:3].bitcast(I32), 0x7F800000, None,
                                      ALU.bitwise_and))
            dve.reciprocal(ws[:, 3:4], ws[:, 2:3]).then_inc(scale_set, 1)
            dve.wait_ge(scale_set, 1)
            for j in range(NC):
                dve.tensor_scalar(us[:, j:j + 1], ws[:, 3:4], UNSCALE / F[j], None, ALU.mult)
            for j in (2, 4):
                dve.tensor_scalar(us[:, NC + j // 2 - 1:NC + j // 2], ws[:, 3:4], -UNSCALE / F[j], None, ALU.mult)
            dve.wait_ge(normed, 4)
            v_single(0, 0, INDEX[("V", 1, 0, 0)])
            for i in range(CT * JT):
                dve.wait_ge(w_hi, i + 1)
                dve.scalar_tensor_tensor(out=W16[:, i // JT, i % JT, WG:2 * WG], in0=w_piece[i], scalar=ws[:, 2:3],
                                         in1=W16[:, i // JT, i % JT, 0:WG], op0=ALU.mult,
                                         op1=ALU.subtract).then_inc(w_lo, 1)
            v_pair(0, 0, INDEX[("V", 1, 0, 1)])
            for c in range(CT):
                if c == CT - 1:
                    stats(1, 1, 0)
                dve.wait_ge(taps_taken, TAKES + TILE_TAKES[c])
                u_pair(0, INDEX[("U", 1, c, 1)], c)
            v_pair(0, 0, INDEX[("V", 1, 0, 3)])
            v_single(0, 0, INDEX[("V", 0, 0, 5)], ahead=1)
            first[0] = steps[0]
            with dve.Fori(0, (N - 2) // 2) as i:
                epoch(i * 2 + 1, 0, True, True)
                epoch(i * 2 + 2, 1, True, True)
            epoch(N - 1, 0, True, False)
            epoch(N, 1, False, False)

        @block.scalar
        def _(act):
            def hi(e, n):
                kind, nxt, c, j = ITEMS[n]
                if n == 0:
                    act.wait_ge(group_done, e * GROUPS)
                elif kind == "V" and nxt == 0:
                    act.wait_ge(group_done, e * GROUPS + CT * (j + 1))
                elif nxt == 1:
                    act.wait_ge(group_done, e * GROUPS + CT * (NC + j + 1))
                if kind == "U" and j == 0:
                    act.wait_ge(taps_taken, e * TAKES + TAKES + TILE_TAKES[c])
                if buffered(ITEMS[n]):
                    act.wait_ge(comp_ready, e * NE + E_INDEX[n] + 1)
                if kind == "V":
                    for t in range(CT):
                        ins = act.copy(comp_out(j, 0, t), tile_rows(E[:, E_INDEX[n] % EB, t * U:(t + 1) * U]))
                else:
                    src = halves(E[:, E_INDEX[n] % EB, :]) if buffered(ITEMS[n]) else G[:, c, :, 0 if j == 0 else 2, :]
                    ins = act.copy(u_flat(j, 0, c), src)
                ins.then_inc(hi_done, 1)

            def take(e, k, o):
                g = CT * k + o
                act.wait_ge(group_done, e * GROUPS + g + 1)
                act.wait_ge(rows_added, e * len(PAIRS) + PAIRS.index((k + 1, o)) + 1 - CT)
                act.activation(DIF[:, o, :], pM[:, g % BANKS, 0:U], ACT.Identity,
                               scale=us[:, k % NC:k % NC + 1]).then_inc(act_took, 1)

            def take_taps(e, u):
                if u == 0:
                    act.wait_ge(lo_done, e * NI + INDEX[("U", 0, CT - 1, 5)] + 1)
                for m in range(MIX_BANKS * u, MIX_BANKS * (u + 1)):
                    act.wait_ge(mixed, e * TAKES + m + 1)
                    src = pG[:, m % MIX_BANKS, :]
                    if m == FULL:
                        src = src.rearrange("p (c n) -> p c n", c=CT)
                    act.mul(mix_part(G[:, :, :, :, :].rearrange("p c o k n -> p c (o k n)"), m), src,
                            MIX_SCALE).then_inc(taps_taken, 1)

            def restore(e, b, n, first, last):
                act.wait_ge(comp_ready, e * NE + E_INDEX[n] + 1)
                for c in range(CT):
                    y = X[b][:, c, first:last, :]
                    act.activation(y, y, ACT.Identity, bias=mean[:, b, c:c + 1],
                                   scale=stdm[:, b, c:c + 1]).then_inc(restored, 1)

            def centre(e, b, chunk):
                act.wait_ge(shift_ready, e + 1)
                for c in range(CT):
                    y = X[b][:, c, 1 + CR * chunk:1 + CR * (chunk + 1), :]
                    act.activation(y, y, ACT.Identity, bias=nmean[:, b, c:c + 1]).then_inc(centred, 1)

            def norm(e, b, chunk):
                act.wait_ge(pooled_ready, e + 1)
                act.wait_ge(centred, e * 4 + CT * (chunk + 1))
                for c in range(CT):
                    y = X[b][:, c, 1 + CR * chunk:1 + CR * (chunk + 1), :]
                    act.activation(y, y, ACT.Copy, scale=rstd[:, c:c + 1]).then_inc(normed, 1)

            def root(e):
                act.wait_ge(var_ready, e + 1)
                act.activation(std0[:, :], var[:, :], ACT.Sqrt).then_inc(std_ready, 1)

            def exponential(e):
                act.wait_ge(logits, e + 1)
                act.activation(ex[:, :], pS[:, 2 * CT:2 * CT + 1], ACT.Exp, bias=nattb[:, 0:1],
                               scale=-1.0).then_inc(exp_ready, 1)

            def restore_chunk_0(e, b):
                restore(e, b, INDEX[("V", 0, 0, 5)], 1, CR)

            def epoch(e, b, more):
                hi(e, INDEX[("V", 0, 0, 5)])
                for c in range(CT):
                    for j in (3, 4):
                        hi(e, INDEX[("U", 0, c, j)])
                for c in range(CT):
                    hi(e, INDEX[("U", 0, c, 5)])
                hi(e, INDEX[("V", 0, 1, 0)])
                restore(e, b, INDEX[("V", 0, 1, 0)], CR, CR + 1)
                take(e, 1, 0)
                take(e, 1, 1)
                take(e, 3, 0)
                if more:
                    centre(e, 1 - b, 0)
                take(e, 3, 1)
                if more:
                    root(e)
                hi(e, INDEX[("V", 0, 1, 1)])
                hi(e, INDEX[("V", 0, 1, 2)])
                if more:
                    centre(e, 1 - b, 1)
                hi(e, INDEX[("V", 0, 1, 3)])
                hi(e, INDEX[("V", 0, 1, 4)])
                if more:
                    exponential(e)
                    norm(e, 1 - b, 0)
                    norm(e, 1 - b, 1)
                restore(e, b, INDEX[("V", 0, 1, 5)], CR + 1, H + 1)
                if more:
                    take_taps(e, 0)
                hi(e, INDEX[("V", 0, 1, 5)])
                if more:
                    hi(e, INDEX[("V", 1, 0, 0)])
                take(e, 7, 0)
                if more:
                    take_taps(e, 1)
                take(e, 7, 1)
                if more:
                    take_taps(e, 2)
                    for c in range(CT):
                        hi(e, INDEX[("U", 1, c, 0)])
                    for j in (1, 2):
                        hi(e, INDEX[("V", 1, 0, j)])
                    for c in range(CT):
                        for j in (1, 2):
                            hi(e, INDEX[("U", 1, c, j)])
                take(e, 9, 0)
                take(e, 9, 1)
                if more:
                    for j in (3, 4):
                        hi(e, INDEX[("V", 1, 0, j)])
                    restore_chunk_0(e + 1, 1 - b)

            act.sem_inc(act_took, len(ACT_TAKES))
            act.sem_inc(hi_done, FIRST_NEXT)
            act.sem_inc(restored, 6)
            act.sem_inc(taps_taken, TAKES)
            act.wait_ge(small_in, 32)
            act.mul(nattb[:, :], attb[:, :], -1.0).then_inc(bias_set, 1)
            root(0)
            for chunk in range(CH):
                centre(0, 0, chunk)
            act.wait_ge(bias_set, 1)
            exponential(0)
            for chunk in range(CH):
                norm(0, 0, chunk)
            act.wait_ge(scale_set, 1)
            for i in range(CT * JT):
                if i >= 2:
                    act.wait_ge(w_lo, i - 1)
                act.activation(W16[:, i // JT, i % JT, 0:WG], w_piece[i], ACT.Copy,
                               scale=ws[:, 2:3]).then_inc(w_hi, 1)
                if i == CT * JT - 2:
                    take_taps(0, 0)
            hi(0, FIRST_NEXT)
            for u in range(1, MIX_UNITS):
                take_taps(0, u)
                if u == 1:
                    hi(0, FIRST_NEXT + 1)
            for n in range(FIRST_NEXT + 2, NI):
                hi(0, n)
            restore_chunk_0(1, 0)
            with act.Fori(0, (N - 2) // 2) as i:
                epoch(i * 2 + 1, 0, True)
                epoch(i * 2 + 2, 1, True)
            epoch(N - 1, 0, True)
            epoch(N, 1, False)

        @block.gpsimd
        def _(pool):
            def lo(e, n):
                kind, nxt, c, j = ITEMS[n]
                pool.wait_ge(hi_done, e * NI + n + 1)
                if kind == "V":
                    for t in range(CT):
                        ins = pool.tensor_tensor(comp_out(j, 1, t), tile_rows(E[:, E_INDEX[n] % EB, t * U:(t + 1) * U]),
                                                 comp_out(j, 0, t), ALU.subtract)
                else:
                    src = halves(E[:, E_INDEX[n] % EB, :]) if buffered(ITEMS[n]) else G[:, c, :, 0 if j == 0 else 2, :]
                    ins = pool.tensor_tensor(u_flat(j, 1, c), src, u_flat(j, 0, c), ALU.subtract)
                ins.then_inc(lo_done, 1)

            def add(e, b, k, o):
                pool.wait_ge(dve_took, e * len(DVE_TAKES) + DVE_TAKES.index((k, o)) + 1)
                if k % NC == 4:
                    pool.wait_ge(row0_added, e * len(PAIRS) + PAIRS.index((k, o)) + 1 - CT)
                y = out_rows(b, k // NC, o, 0)
                pool.tensor_tensor(y, y, tile_rows(SUM[:, o, :]), ALU.add).then_inc(row0_added, 1)

            def epoch(e, b, more):
                def items(first, last):
                    for n in range(INDEX[first], INDEX[last] + 1):
                        lo(e, n)

                items(("V", 0, 0, 5), ("V", 0, 1, 0))
                add(e, b, 2, 0)
                add(e, b, 2, 1)
                items(("V", 0, 1, 1), ("V", 0, 1, 3))
                add(e, b, 4, 0)
                items(("V", 0, 1, 4), ("V", 0, 1, 4))
                add(e, b, 4, 1)
                items(("V", 0, 1, 5), ("V", 0, 1, 5))
                if more:
                    items(("V", 1, 0, 0), ("V", 1, 0, 1))
                add(e, b, 8, 0)
                if more:
                    items(("V", 1, 0, 2), ("V", 1, 0, 2))
                add(e, b, 8, 1)
                if more:
                    items(("U", 1, 0, 1), ("V", 1, 0, 3))
                add(e, b, 10, 0)
                if more:
                    items(("V", 1, 0, 4), ("V", 1, 0, 4))
                add(e, b, 10, 1)

            pool.sem_inc(lo_done, FIRST_NEXT)
            pool.sem_inc(row0_added, len(PAIRS))
            pool.memset(sel[:, :], 0.0).then_inc(pool_step, 1)
            pool.wait_ge(pool_step, 1)
            for k in range(K):
                pool.affine_select(out=sel[:, :], in_=sel[:, :], compare_op=ALU.not_equal, fill=1.0, base=-CI * k,
                                   pattern=[[-1, CI]], channel_multiplier=1).then_inc(pool_step, 1)
                pool.wait_ge(pool_step, k + 2)
            blocks = avg[:, :].rearrange("p (g j) -> p g j", j=GS)
            pool.memset(avg[:, :], 1.0 / GS).then_inc(pool_step, 1)
            pool.wait_ge(pool_step, K + 2)
            pool.affine_select(out=blocks, in_=blocks, compare_op=ALU.is_ge, fill=0.0, base=0,
                               pattern=[[-GS, P // GS], [0, GS]], channel_multiplier=1).then_inc(pool_step, 1)
            pool.wait_ge(pool_step, K + 3)
            pool.affine_select(out=blocks, in_=blocks, compare_op=ALU.is_ge, fill=0.0, base=GS - 1,
                               pattern=[[GS, P // GS], [0, GS]], channel_multiplier=-1).then_inc(avg_set, 1)
            pool.wait_ge(w_top, 1)
            pool.partition_all_reduce(wall[:, :], wtop[:, :], P, bass.bass_isa.ReduceOp.max).then_inc(w_all, 1)
            for n in range(FIRST_NEXT, NI):
                lo(0, n)
            with pool.Fori(0, (N - 2) // 2) as i:
                epoch(i * 2 + 1, 0, True)
                epoch(i * 2 + 2, 1, True)
            epoch(N - 1, 0, True)
            epoch(N, 1, False)


def kernel(x, L0_conv_weight, L0_conv_att_w, L0_conv_att_b):
    import numpy as np
    import concourse.bacc as bacc
    from concourse.bass_utils import run_bass_kernel_spmd

    nc = bacc.Bacc("TRN2", target_bir_lowering=False, num_devices=1, dynamic_dma_scratch_size=16)
    w = np.ascontiguousarray(L0_conv_weight).reshape(K, CT, P, CT, JT, CI, KS, KS)
    w = np.ascontiguousarray(w.transpose(0, 5, 3, 4, 1, 6, 7, 2)).reshape(P, CT * JT, WG)
    arrays = {
        "x_dram": np.ascontiguousarray(x),
        "w_dram": w,
        "attw_dram": np.repeat(np.ascontiguousarray(L0_conv_att_w).T, CI, axis=1),
        "attb_dram": np.repeat(np.ascontiguousarray(L0_conv_att_b), CI).reshape(P, 1),
    }
    args = [nc.dram_tensor(n, a.shape, F32, kind="ExternalInput").ap() for n, a in arrays.items()]
    args.append(nc.dram_tensor("out_dram", (N, C, H, W), F32, kind="ExternalOutput").ap())
    conv_kernel(nc, *args)
    return run_bass_kernel_spmd(nc, [arrays], core_ids=[0]).results[0]["out_dram"]
```
